# Optimizing a Trainium2 kernel written in Bass

```python
import numpy as np
import jax
import jax.numpy as jnp

def _softmax(x, axis=-1):
    return jax.nn.softmax(x, axis=axis)

def _gelu(x):
    return jax.nn.gelu(x, approximate=True)

def _silu(x):
    return jax.nn.silu(x)

def _sigmoid(x):
    return jax.nn.sigmoid(x)

def _layernorm(x, axis=-1, eps=1e-05):
    m = jnp.mean(x, axis=axis, keepdims=True)
    v = jnp.var(x, axis=axis, keepdims=True)
    return (x - m) / jnp.sqrt(v + eps)

def _scatter_add(tgt, idx, src, axis=0):
    return tgt.at[idx].add(src)

def _segment_sum(src, seg, n):
    return jax.ops.segment_sum(src, seg, n)
kernel_name = 'mk_decoder_postln_d1_seqx_r8_c7ff98'

def setup_inputs(seed: int=0):
    np.random.seed(seed)
    _w = jnp.asarray

    def _rec_inputs():
        import jax
        import jax.numpy as jnp
        _rk = jax.random.key(seed)
        x = -0.0002928 + 1 * jax.random.normal(jax.random.fold_in(_rk, 1), (16, 64, 128), jnp.float32)
        _lenS = 64 - jax.random.randint(jax.random.fold_in(_rk, 7), (16,), 0, max(1, 64 // 4) + 1, jnp.int32)
        _lenS2 = 64 - jax.random.randint(jax.random.fold_in(_rk, 8), (16,), 0, max(1, 64 // 4) + 1, jnp.int32)
        _ctx_1024P = jax.random.normal(jax.random.fold_in(_rk, 11), (16, 16, 128), jnp.float32)
        _ctx_1024c = jax.random.dirichlet(jax.random.fold_in(_rk, 511), 0.3 * jnp.ones((16,), jnp.float32), (16, 64))
        _ctx_1024t = jnp.einsum('bsk,bkd->bsd', _ctx_1024c, _ctx_1024P)
        _ctx_1024t = _ctx_1024t * jax.lax.rsqrt(jnp.mean(jnp.square(_ctx_1024t)) + 1e-12) * 0.953939
        ctx_1024 = -1.39393e-06 + 0.999914 * (_ctx_1024t + 0.3 * jax.random.normal(jax.random.fold_in(_rk, 611), (16, 64, 128), jnp.float32))
        return (x, ctx_1024)
    x, ctx_1024 = _rec_inputs()

    def _L0_attn_setup():
        import jax, jax.numpy as jnp
        import numpy as np
        D_MODEL = 128
        D_INNER = 256
        D_STATE = 16
        D_CONV = 4
        DT_RANK = 128
        BATCH = 4
        SEQ = 256

        def silu(x):
            return x * jax.nn.sigmoid(x)

        def causal_depthwise_conv(x, w, b):
            lhs = jnp.moveaxis(x, 1, 2)
            rhs = w[:, None, :]
            y = jax.lax.conv_general_dilated(lhs, rhs, window_strides=(1,), padding=[(D_CONV - 1, 0)], dimension_numbers=('NCH', 'OIH', 'NCH'), feature_group_count=x.shape[-1])
            return jnp.moveaxis(y, 2, 1) + b

        def selective_scan(delta, Bm, Cm, u, A):
            dT = jnp.moveaxis(delta, 1, 0)
            BT = jnp.moveaxis(Bm, 1, 0)
            CT = jnp.moveaxis(Cm, 1, 0)
            uT = jnp.moveaxis(u, 1, 0)
            h0 = jnp.zeros((delta.shape[0], delta.shape[2], A.shape[1]), delta.dtype)

            def step(h, ins):
                d_t, B_t, C_t, u_t = ins
                h = jnp.exp(d_t[..., None] * A) * h + (d_t * u_t)[..., None] * B_t[:, None, :]
                y = jnp.einsum('bdn,bn->bd', h, C_t)
                return (h, y)
            _, yT = jax.lax.scan(step, h0, (dT, BT, CT, uT))
            return jnp.moveaxis(yT, 0, 1)
        key = jax.random.key(seed)
        ks = jax.random.split(key, 10)
        s = 0.02
        return {'x': jax.random.normal(ks[0], (BATCH, SEQ, D_MODEL), jnp.float32), 'W_in_o': jax.random.normal(ks[1], (D_MODEL, 2 * D_INNER), jnp.float32) * s, 'b_in_o': jnp.zeros((2 * D_INNER,), jnp.float32), 'W_out_o': jax.random.normal(ks[2], (D_INNER, D_MODEL), jnp.float32) * s, 'b_out_o': jnp.zeros((D_MODEL,), jnp.float32), 'W_in_i': jax.random.normal(ks[3], (D_INNER, 2 * D_INNER), jnp.float32) * s, 'conv_w': jax.random.normal(ks[4], (D_INNER, D_CONV), jnp.float32) * s, 'conv_b': jnp.zeros((D_INNER,), jnp.float32), 'W_xp': jax.random.normal(ks[5], (D_INNER, DT_RANK + 2 * D_STATE), jnp.float32) * s, 'W_dt': jax.random.normal(ks[6], (DT_RANK, D_INNER), jnp.float32) * s, 'b_dt': jnp.log(jnp.expm1(jax.random.uniform(ks[7], (D_INNER,), jnp.float32, 0.001, 0.1))), 'A_log': jnp.log(jnp.broadcast_to(jnp.arange(1, D_STATE + 1, dtype=jnp.float32), (D_INNER, D_STATE))), 'D_skip': jnp.ones((D_INNER,), jnp.float32), 'W_out_i': jax.random.normal(ks[8], (D_INNER, D_INNER), jnp.float32) * s}
    _L0_attn_all = _L0_attn_setup()
    _L0_attn_in = {k: v for k, v in _L0_attn_all.items() if k in ('W_in_o', 'b_in_o', 'W_out_o', 'b_out_o', 'W_in_i', 'conv_w', 'conv_b', 'W_xp', 'W_dt', 'b_dt', 'A_log', 'D_skip', 'W_out_i')}
    del _L0_attn_all

    def _L0_xattn_setup():
        import jax, jax.numpy as jnp
        import numpy as np
        D_MODEL = 128
        N_HEADS = 16
        D_K = D_MODEL // N_HEADS
        EPS = 1e-08

        def _l2_rownorm(x):
            return x * jax.lax.rsqrt(jnp.sum(x * x, axis=-1, keepdims=True) + EPS)
        key = jax.random.key(seed)
        ks = jax.random.split(key, 11)
        B, S = (2, 256)
        sc = 1.0 / np.sqrt(D_MODEL)
        inp = {'Q': jax.random.normal(ks[0], (B, S, D_MODEL), jnp.float32), 'K': jax.random.normal(ks[1], (B, S, D_MODEL), jnp.float32), 'V': jax.random.normal(ks[2], (B, S, D_MODEL), jnp.float32), 'Wq_w': jax.random.normal(ks[3], (D_MODEL, D_MODEL), jnp.float32) * sc, 'Wq_b': jnp.zeros((D_MODEL,), jnp.float32), 'Wk_w': jax.random.normal(ks[4], (D_MODEL, D_MODEL), jnp.float32) * sc, 'Wk_b': jnp.zeros((D_MODEL,), jnp.float32), 'Wv_w': jax.random.normal(ks[5], (D_MODEL, D_MODEL), jnp.float32) * sc, 'Wv_b': jnp.zeros((D_MODEL,), jnp.float32), 'Wo_w': jax.random.normal(ks[6], (D_MODEL, D_MODEL), jnp.float32) * sc, 'Wo_b': jnp.zeros((D_MODEL,), jnp.float32)}
        return inp
    _L0_xattn_all = _L0_xattn_setup()
    _L0_xattn_in = {k: v for k, v in _L0_xattn_all.items() if k in ('Wq_w', 'Wq_b', 'Wk_w', 'Wk_b', 'Wv_w', 'Wv_b', 'Wo_w', 'Wo_b')}
    del _L0_xattn_all

    def _L0_ffn_setup():
        import jax, jax.numpy as jnp
        import numpy as np
        D_IN, D_HID = (128, 512)

        def _ternary(key, shape):
            return jax.random.randint(key, shape, -1, 2).astype(jnp.float32)

        def _tlin(x, w, s):
            return jnp.einsum('bsi,oi->bso', x, w) * s
        key = jax.random.key(seed)
        ks = jax.random.split(key, 12)
        inv = lambda fan: 1.0 / np.sqrt(fan).astype(np.float32)
        return {'x': jax.random.normal(ks[0], (4, 256, D_IN), dtype=jnp.float32), 'w1_w': _ternary(ks[1], (D_HID, D_IN)), 'w1_s': jax.random.uniform(ks[2], (D_HID,), dtype=jnp.float32) * inv(D_IN), 'w2_w': _ternary(ks[3], (D_HID, D_IN)), 'w2_s': jax.random.uniform(ks[4], (D_HID,), dtype=jnp.float32) * inv(D_IN), 'h1_w': _ternary(ks[5], (D_HID, D_HID)), 'h1_s': jax.random.uniform(ks[6], (D_HID,), dtype=jnp.float32) * inv(D_HID), 'h2_w': _ternary(ks[7], (D_HID, D_HID)), 'h2_s': jax.random.uniform(ks[8], (D_HID,), dtype=jnp.float32) * inv(D_HID), 'w3_w': _ternary(ks[9], (D_IN, D_HID)), 'w3_s': jax.random.uniform(ks[10], (D_IN,), dtype=jnp.float32) * inv(D_HID)}
    _L0_ffn_all = _L0_ffn_setup()
    _L0_ffn_in = {k: v for k, v in _L0_ffn_all.items() if k in ('w1_w', 'w1_s', 'w2_w', 'w2_s', 'h1_w', 'h1_s', 'h2_w', 'h2_s', 'w3_w', 'w3_s')}
    del _L0_ffn_all
    return {'x': x, 'ctx_1024': ctx_1024, 'L0_attn_W_in_o': _L0_attn_in['W_in_o'], 'L0_attn_b_in_o': _L0_attn_in['b_in_o'], 'L0_attn_W_out_o': _L0_attn_in['W_out_o'], 'L0_attn_b_out_o': _L0_attn_in['b_out_o'], 'L0_attn_W_in_i': _L0_attn_in['W_in_i'], 'L0_attn_conv_w': _L0_attn_in['conv_w'], 'L0_attn_conv_b': _L0_attn_in['conv_b'], 'L0_attn_W_xp': _L0_attn_in['W_xp'], 'L0_attn_W_dt': _L0_attn_in['W_dt'], 'L0_attn_b_dt': _L0_attn_in['b_dt'], 'L0_attn_A_log': _L0_attn_in['A_log'], 'L0_attn_D_skip': _L0_attn_in['D_skip'], 'L0_attn_W_out_i': _L0_attn_in['W_out_i'], 'L0_xattn_Wq_w': _L0_xattn_in['Wq_w'], 'L0_xattn_Wq_b': _L0_xattn_in['Wq_b'], 'L0_xattn_Wk_w': _L0_xattn_in['Wk_w'], 'L0_xattn_Wk_b': _L0_xattn_in['Wk_b'], 'L0_xattn_Wv_w': _L0_xattn_in['Wv_w'], 'L0_xattn_Wv_b': _L0_xattn_in['Wv_b'], 'L0_xattn_Wo_w': _L0_xattn_in['Wo_w'], 'L0_xattn_Wo_b': _L0_xattn_in['Wo_b'], 'L0_ffn_w1_w': _L0_ffn_in['w1_w'], 'L0_ffn_w1_s': _L0_ffn_in['w1_s'], 'L0_ffn_w2_w': _L0_ffn_in['w2_w'], 'L0_ffn_w2_s': _L0_ffn_in['w2_s'], 'L0_ffn_h1_w': _L0_ffn_in['h1_w'], 'L0_ffn_h1_s': _L0_ffn_in['h1_s'], 'L0_ffn_h2_w': _L0_ffn_in['h2_w'], 'L0_ffn_h2_s': _L0_ffn_in['h2_s'], 'L0_ffn_w3_w': _L0_ffn_in['w3_w'], 'L0_ffn_w3_s': _L0_ffn_in['w3_s']}

def reference(x, ctx_1024, L0_attn_W_in_o, L0_attn_b_in_o, L0_attn_W_out_o, L0_attn_b_out_o, L0_attn_W_in_i, L0_attn_conv_w, L0_attn_conv_b, L0_attn_W_xp, L0_attn_W_dt, L0_attn_b_dt, L0_attn_A_log, L0_attn_D_skip, L0_attn_W_out_i, L0_xattn_Wq_w, L0_xattn_Wq_b, L0_xattn_Wk_w, L0_xattn_Wk_b, L0_xattn_Wv_w, L0_xattn_Wv_b, L0_xattn_Wo_w, L0_xattn_Wo_b, L0_ffn_w1_w, L0_ffn_w1_s, L0_ffn_w2_w, L0_ffn_w2_s, L0_ffn_h1_w, L0_ffn_h1_s, L0_ffn_h2_w, L0_ffn_h2_s, L0_ffn_w3_w, L0_ffn_w3_s):
    import jax
    import jax.numpy as jnp

    def _L0_attn_ref(x, W_in_o, b_in_o, W_out_o, b_out_o, W_in_i, conv_w, conv_b, W_xp, W_dt, b_dt, A_log, D_skip, W_out_i):
        import jax, jax.numpy as jnp
        import numpy as np
        D_MODEL = 128
        D_INNER = 256
        D_STATE = 16
        D_CONV = 4
        DT_RANK = 128
        BATCH = 4
        SEQ = 256

        def silu(x):
            return x * jax.nn.sigmoid(x)

        def causal_depthwise_conv(x, w, b):
            lhs = jnp.moveaxis(x, 1, 2)
            rhs = w[:, None, :]
            y = jax.lax.conv_general_dilated(lhs, rhs, window_strides=(1,), padding=[(D_CONV - 1, 0)], dimension_numbers=('NCH', 'OIH', 'NCH'), feature_group_count=x.shape[-1])
            return jnp.moveaxis(y, 2, 1) + b

        def selective_scan(delta, Bm, Cm, u, A):
            dT = jnp.moveaxis(delta, 1, 0)
            BT = jnp.moveaxis(Bm, 1, 0)
            CT = jnp.moveaxis(Cm, 1, 0)
            uT = jnp.moveaxis(u, 1, 0)
            h0 = jnp.zeros((delta.shape[0], delta.shape[2], A.shape[1]), delta.dtype)

            def step(h, ins):
                d_t, B_t, C_t, u_t = ins
                h = jnp.exp(d_t[..., None] * A) * h + (d_t * u_t)[..., None] * B_t[:, None, :]
                y = jnp.einsum('bdn,bn->bd', h, C_t)
                return (h, y)
            _, yT = jax.lax.scan(step, h0, (dT, BT, CT, uT))
            return jnp.moveaxis(yT, 0, 1)
        xz = x @ W_in_o + b_in_o
        x_proj, z_proj = (xz[..., :D_INNER], xz[..., D_INNER:])
        xz2 = x_proj @ W_in_i
        xm, zm = (xz2[..., :D_INNER], xz2[..., D_INNER:])
        xc = silu(causal_depthwise_conv(xm, conv_w, conv_b))
        dbl = xc @ W_xp
        dt = dbl[..., :DT_RANK]
        Bm = dbl[..., DT_RANK:DT_RANK + D_STATE]
        Cm = dbl[..., DT_RANK + D_STATE:]
        delta = jax.nn.softplus(dt @ W_dt + b_dt)
        A = -jnp.exp(A_log)
        y = selective_scan(delta, Bm, Cm, xc, A) + D_skip * xc
        y = y * silu(zm)
        out_i = y @ W_out_i
        out = out_i * jax.nn.sigmoid(z_proj)
        return out @ W_out_o + b_out_o

    def _L0_xattn_ref(Q, K, V, Wq_w, Wq_b, Wk_w, Wk_b, Wv_w, Wv_b, Wo_w, Wo_b):
        import jax, jax.numpy as jnp
        import numpy as np
        D_MODEL = 128
        N_HEADS = 16
        D_K = D_MODEL // N_HEADS
        EPS = 1e-08

        def _l2_rownorm(x):
            return x * jax.lax.rsqrt(jnp.sum(x * x, axis=-1, keepdims=True) + EPS)
        B, S, _ = Q.shape
        q = (Q @ Wq_w.T + Wq_b).reshape(B, S, N_HEADS, D_K).transpose(0, 2, 1, 3)
        k = (K @ Wk_w.T + Wk_b).reshape(B, S, N_HEADS, D_K).transpose(0, 2, 1, 3)
        v = (V @ Wv_w.T + Wv_b).reshape(B, S, N_HEADS, D_K).transpose(0, 2, 1, 3)
        qn = _l2_rownorm(q)
        kn = _l2_rownorm(k)
        scores = jnp.einsum('bhqd,bhkd->bhqk', qn, kn)
        attn = scores * scores
        out = jnp.einsum('bhqk,bhkd->bhqd', attn, v)
        out = out.transpose(0, 2, 1, 3).reshape(B, S, D_MODEL)
        return out @ Wo_w.T + Wo_b

    def _L0_ffn_ref(x, w1_w, w1_s, w2_w, w2_s, h1_w, h1_s, h2_w, h2_s, w3_w, w3_s):
        import jax, jax.numpy as jnp
        import numpy as np
        D_IN, D_HID = (128, 512)

        def _ternary(key, shape):
            return jax.random.randint(key, shape, -1, 2).astype(jnp.float32)

        def _tlin(x, w, s):
            return jnp.einsum('bsi,oi->bso', x, w) * s
        h = jax.nn.silu(_tlin(x, w1_w, w1_s)) * _tlin(x, w2_w, w2_s)
        h = jax.nn.gelu(_tlin(h, h1_w, h1_s), approximate=False)
        h = jax.nn.gelu(_tlin(h, h2_w, h2_s), approximate=False)
        return _tlin(h, w3_w, w3_s)
    x = _layernorm(x + _L0_attn_ref(x, L0_attn_W_in_o, L0_attn_b_in_o, L0_attn_W_out_o, L0_attn_b_out_o, L0_attn_W_in_i, L0_attn_conv_w, L0_attn_conv_b, L0_attn_W_xp, L0_attn_W_dt, L0_attn_b_dt, L0_attn_A_log, L0_attn_D_skip, L0_attn_W_out_i), axis=-1)
    x = _layernorm(x + _L0_xattn_ref(x, ctx_1024, ctx_1024, L0_xattn_Wq_w, L0_xattn_Wq_b, L0_xattn_Wk_w, L0_xattn_Wk_b, L0_xattn_Wv_w, L0_xattn_Wv_b, L0_xattn_Wo_w, L0_xattn_Wo_b), axis=-1)
    x = _layernorm(x + _L0_ffn_ref(x, L0_ffn_w1_w, L0_ffn_w1_s, L0_ffn_w2_w, L0_ffn_w2_s, L0_ffn_h1_w, L0_ffn_h1_s, L0_ffn_h2_w, L0_ffn_h2_s, L0_ffn_w3_w, L0_ffn_w3_s), axis=-1)
    return x

_drawn_inputs = setup_inputs


def setup_inputs(seed=0):
    import zlib

    import numpy as np

    out = dict(_drawn_inputs(seed))
    spreads = {'L0_attn_b_in_o': (0.0, 0.8),
     'L0_attn_b_out_o': (0.0, 0.8),
     'L0_attn_conv_b': (0.0, 0.8),
     'L0_attn_D_skip': (1.0, 0.6),
     'L0_xattn_Wq_b': (0.0, 0.1),
     'L0_xattn_Wk_b': (0.0, 0.1),
     'L0_xattn_Wv_b': (0.0, 0.1),
     'L0_xattn_Wo_b': (0.0, 0.344)}
    factors = {'L0_attn_W_in_o': 8.0,
     'L0_attn_W_out_o': 8.0,
     'L0_attn_W_in_i': 8.0,
     'L0_attn_conv_w': 8.0,
     'L0_attn_W_xp': 8.0,
     'L0_attn_W_dt': 8.0,
     'L0_attn_b_dt': 8.0,
     'L0_attn_A_log': 8.0,
     'L0_attn_W_out_i': 8.0,
     'L0_ffn_w1_w': 8.0,
     'L0_ffn_w1_s': 8.0,
     'L0_ffn_w2_w': 8.0,
     'L0_ffn_w2_s': 8.0,
     'L0_ffn_h1_w': 8.0,
     'L0_ffn_h1_s': 8.0,
     'L0_ffn_h2_w': 8.0,
     'L0_ffn_h2_s': 8.0,
     'L0_ffn_w3_w': 8.0,
     'L0_ffn_w3_s': 8.0}
    for name, (base, spread) in spreads.items():
        noise = np.random.default_rng([zlib.crc32(name.encode()), seed]).standard_normal(out[name].shape)
        drawn = base * np.exp(spread * noise) if base else spread * noise
        out[name] = jnp.asarray(drawn.astype(out[name].dtype))
    for name, factor in factors.items():
        out[name] = (out[name] * factor).astype(out[name].dtype)
    return out
```

```python
from contextlib import ExitStack

import concourse.bass as bass
from concourse import mybir
import numpy as np

ALU = mybir.AluOpType
ACT = mybir.ActivationFunctionType
F32 = mybir.dt.float32
BF16 = mybir.dt.bfloat16

P = 128
BATCH, SEQ = 16, 64
TOKENS = BATCH * SEQ
BLOCKS = 2
T = TOKENS // BLOCKS
SEQS = T // SEQ
PAIRS = SEQS // 2
TILES = T // P
INNER = 256
CH = INNER // P
STATES = 16
TAPS = 4
HEADS, DK = 16, 8
HG, HI = 4, 4
HID = 512
FT = HID // P
VROW = HI * (32 + DK)
PARTS = 3
BC = 2 * STATES
WORK_BANKS = 3
RING = 4
DA_RING = 2
CS_RING = 3
LAG = 3
POOL_STATES = (0, 1, 3, 4, 6, 7, 9, 10, 12, 13, 15)

MATS = [("win_xT", CH * P), ("win_i", CH * 2 * INNER), ("wxpT", INNER), ("wdt", INNER), ("win_z", INNER),
        ("wbc", CH * PARTS * BC), ("ident", P), ("mean", P), ("ones", P), ("headsel", HEADS),
        ("wkT", P), ("wvT", P), ("wouti", CH * INNER), ("wouto", CH * P), ("wqT", P), ("woT", P),
        ("w1T", HID), ("w2T", HID), ("h1T", FT * HID), ("h2T", FT * HID), ("w3T", FT * P)]
VECS = [("b_x", CH), ("b_z", CH), ("conv_w", CH * TAPS), ("conv_b", CH), ("b_dt", CH), ("a_log", CH * STATES),
        ("d_skip", CH), ("b_out", 1), ("bq", 1), ("bk", 1), ("bo", 1), ("s1", FT), ("s2", FT), ("h1s", FT),
        ("h2s", FT), ("s3", 1), ("hmask", HI), ("eps", 1), ("sel", BC)]
LN_EPS, L2_EPS = 1e-5, 1e-8


def columns(parts):
    at, n = {}, 0
    for name, w in parts:
        at[name] = (n, n + w)
        n += w
    return at, n


MAT_AT, MAT_COLS = columns(MATS)
VEC_AT, VEC_COLS = columns(VECS)
LOADS = [("win_xT", "wdt"), ("win_z", "headsel"), ("wkT", "wvT"), ("wouti", "woT"), ("w1T", "w3T")]


def schedule():
    steps = [("prep",), ("front_conv", 0), ("front_gates", 0), ("front_delta", 0)]
    fill = {0: [("front_conv", 1), ("front_gates", 1), ("front_delta", 1), ("keys", 0), ("values", 0)],
            1: [("mamba_out", 0), ("norm", 0, 1), ("query", 0)] + [("attend", 0, p) for p in range(PAIRS + 1)]
            + [("attn_out", 0), ("norm", 0, 2), ("keys", 1), ("values", 1)]
            + [("gate_up", 0, j) for j in range(FT)] + [("hid1", 0, j) for j in range(FT)]
            + [("hid2", 0, j) for j in range(FT)] + [("down", 0), ("norm", 0, 3), ("store", 0)]}
    at = {0: (2, 14), 1: (STATES + LAG, 2 * STATES + LAG)}
    total = BLOCKS * STATES + LAG
    for s in range(total):
        for b, (a, z) in at.items():
            n = len(fill[b])
            if a <= s < z:
                steps += fill[b][n * (s - a) // (z - a):n * (s - a + 1) // (z - a)]
        steps.append(("scan", s))
    b = 1
    steps += [("mamba_out", b), ("norm", b, 1), ("query", b)] + [("attend", b, p) for p in range(PAIRS + 1)]
    steps += [("attn_out", b), ("norm", b, 2)] + [("gate_up", b, j) for j in range(FT)]
    steps += [("hid1", b, j) for j in range(FT)] + [("hid2", b, j) for j in range(FT)]
    steps += [("down", b), ("norm", b, 3), ("store", b)]
    return steps


def work_tiles(step):
    kind, *at = step
    b = at[0] if at else 0
    if kind == "prep":
        return [(("wf",), "act"), (("wxd",), "act"), (("bf",), "dve")]
    if kind == "front_conv":
        return [(("xm", b, c), "act") for c in range(CH)]
    if kind == "front_gates":
        return [((k, b, c), "act") for k in ("zm", "z") for c in range(CH)]
    if kind == "front_delta":
        return [(("dl", b, c), "act") for c in range(CH)] + [(("bc", b), "dve")]
    if kind == "keys":
        return [(("k", b), "act"), (("ssk", b), "dve")]
    if kind == "values":
        return [(("v", b), "dve")]
    if kind == "mamba_out":
        return [(("oi", b, c), "dve") for c in range(CH)] + [(("oo", b), "dve")]
    if kind == "norm":
        return [(("mu", *at), "dve"), (("var", *at), "act"), (("rb", *at), "dve")]
    if kind == "query":
        return [(("q", b), "act"), (("ssq", b), "dve"), (("rqb", b), "act")]
    if kind == "attend":
        p = at[1]
        return [(("s", b, p, n), "act") for n in range(2) if p < PAIRS] + [(("o", b, p - 1), "dve")] * (p > 0)
    if kind == "attn_out":
        return [(("wo", b), "dve")]
    if kind == "gate_up":
        return [(("w1", *at), "act"), (("w2", *at), "dve")]
    if kind == "hid1":
        return [(("h1", *at), "act")]
    if kind == "hid2":
        return [(("h2", *at), "act")]
    if kind == "down":
        return [(("w3", b), "dve")]
    return []


def decoder_layer(nc, xT, ctxT, mats, vecs, bv, out):
    steps = schedule()
    work = [w for step in steps for w in work_tiles(step)]
    number = {key: n for n, (key, _) in enumerate(work)}
    emptied = [sum(e == engine for _, e in work[:n + 1]) for n, (_, engine) in enumerate(work)]

    with ExitStack() as ctx:
        def sb(name, shape, dt=F32):
            return ctx.enter_context(nc.sbuf_tensor(name, [P, *shape], dt))

        def psum(name, shape):
            return ctx.enter_context(nc.psum_tensor(name, [P, *shape], F32))

        def sem(name):
            return ctx.enter_context(nc.semaphore(name))

        mat = sb("mat", [MAT_COLS])
        vec = sb("vec", [VEC_COLS])
        bv_row = sb("bv_row", [P])
        x = sb("x", [TOKENS])
        kv = sb("kv", [TOKENS])
        wf = sb("wf", [2 * INNER])
        wxd = sb("wxd", [CH, INNER])
        bf = sb("bf", [2 * CH])
        hbz = sb("hbz", [CH])
        neg_a = sb("neg_a", [CH * STATES])
        selb = sb("selb", [BC, P], BF16)
        xpad = sb("xpad", [CH, SEQS, TAPS - 1 + SEQ])
        xc, zgate, mgate, delta, du = ([sb(f"{n}{b}", [CH, T]) for b in range(BLOCKS)]
                                       for n in ("xc", "zgate", "mgate", "delta", "du"))
        parts = [sb(f"parts{b}", [T], BF16) for b in range(BLOCKS)]
        mid = sb("mid", [T], BF16)
        decay = [sb(f"decay{i}", [CH, T]) for i in range(DA_RING)]
        state = [sb(f"state{i}", [CH, T]) for i in range(RING)]
        c_all = [sb(f"c_all{i}", [T]) for i in range(CS_RING)]
        kmask = sb("kmask", [HG, T])
        vmask = sb("vmask", [PAIRS, 2, HG, VROW])
        ssk, rk, ssq, rq = (sb(n, [TILES, HEADS]) for n in ("ssk", "rk", "ssq", "rq"))
        hid_a = sb("hid_a", [FT, T])
        hid_b = sb("hid_b", [FT, T])
        hid_c = sb("hid_c", [FT, T])
        y, dev, sq, x1, x2, diag = (sb(n, [T]) for n in ("y", "dev", "sq", "x1", "x2", "diag"))
        std, rstd = sb("std", [TILES]), sb("rstd", [TILES])
        up = sb("up", [T])
        rest = up
        final = x1
        attn1 = sb("attn1", [HEADS * SEQ])
        conv = hid_c[:, 0:CH, :]
        pre, expo, logt, trunc = hid_a[:, 0:2, :], hid_a[:, 2:4, :], hid_b[:, 0:2, :], hid_b[:, 2:4, :]
        gated = hid_a[:, 2:4, :]
        q, q2, heads_out, rq_all, rq_wide = (hid_b[:, 0, :], hid_b[:, 1, :], hid_b[:, 2, :], hid_b[:, 3, :],
                                             hid_a[:, 0, :])
        qmask = hid_c

        def m(name):
            return mat[:, MAT_AT[name][0]:MAT_AT[name][1]]

        def v(name):
            return vec[:, VEC_AT[name][0]:VEC_AT[name][1]]

        attn = [m("win_i"), attn1]
        ident, mean, ones = m("ident"), m("mean"), m("ones")

        b_all = psum("b_all", [2, T])
        c_psum = psum("c_psum", [T])
        y_sum = psum("y_sum", [CH, T])
        bank = [psum(f"work{i}", [T]) for i in range(WORK_BANKS)]

        loaded = {n: sem(f"loaded_{n}") for n in ("vec", "x", "kv", "bv", *(a for a, _ in LOADS))}
        filled = sem("work_filled")
        used = {"act": sem("work_used_by_act"), "dve": sem("work_used_by_dve")}
        zeroed = sem("zeroed")
        small = sem("small_ready")
        a_exp = sem("a_exp_ready")
        conv_step = sem("conv_step")
        xc_ready = sem("xc_ready")
        soft_act = sem("softplus_act_step")
        soft_dve = sem("softplus_dve_step")
        split = sem("split_step")
        b_ready, c_ready = sem("b_ready"), sem("c_ready")
        decay_ready = sem("decay_ready")
        c_copied = sem("c_copied")
        in_ready = sem("scan_input_ready")
        scanned = sem("scanned")
        hc_dve, hc_pool = sem("output_product_dve"), sem("output_product_pool")
        summed = sem("summed")
        rk_ready = sem("rk_ready")
        y_out = sem("mamba_y_step")
        k_ready = sem("masked_keys_ready")
        res_ready = sem("residual_ready")
        sq_ready = sem("squares_ready")
        norm_dve = sem("norm_dve_step")
        q_ready = sem("q_ready")
        qm_ready = sem("qmask_ready")
        rq_step = sem("rq_step")
        stored = sem("stored")

        block = ctx.enter_context(nc.Block())

        def tile(key):
            return bank[number[key] % WORK_BANKS]

        def wait_emptied(eng, key):
            eng.wait_ge(used[work[number[key]][1]], emptied[number[key]])

        def wait_filled(eng, key):
            eng.wait_ge(filled, number[key] + 1)

        def wait_bank_free(eng, key):
            n = number[key]
            if n >= WORK_BANKS:
                wait_emptied(eng, work[n - WORK_BANKS][0])

        def tok(b):
            return slice(b * T, (b + 1) * T)

        def pool_done(s):
            return sum(n % STATES in POOL_STATES for n in range(s + 1))

        def wait_product(eng, s):
            n = pool_done(s)
            if s % STATES in POOL_STATES:
                eng.wait_ge(hc_pool, n)
            else:
                eng.wait_ge(hc_dve, s + 1 - n)

        @block.sync
        def _(sp):
            def load(name, dst, src):
                sp.dma_start(dst, src).then_inc(loaded[name], 16)

            def load_mats(n):
                a, z = MAT_AT[LOADS[n][0]][0], MAT_AT[LOADS[n][1]][1]
                load(LOADS[n][0], mat[:, a:z], mats[:, a:z])

            load("vec", vec[:, :], vecs)
            load_mats(0)
            load("x", x[:, :], xT)
            load_mats(1)
            load("kv", kv[:, :], ctxT)
            load("bv", bv_row[0:1, :], bv)
            for n in range(2, len(LOADS)):
                load_mats(n)
            for b in range(BLOCKS):
                wait_emptied(sp, ("rb", b, 3))
                sp.dma_start(out[:, tok(b)], final[:, :]).then_inc(stored, 16)
            sp.wait_ge(stored, 16 * BLOCKS)

        def norm_index(b, i):
            return [s for s in steps if s[0] == "norm"].index(("norm", b, i))

        def norm_steps(b, i, n):
            return 2 * norm_index(b, i) + n

        @block.tensor
        def _(pe):
            mm = nc.tensor.matmul

            def wait_mats(*names):
                for n in names:
                    pe.wait_ge(loaded[n], 16)

            def prep():
                wait_mats("win_xT")
                out_ = tile(("wf",))
                wxT, wi = m("win_xT").rearrange("p (k n) -> p k n", k=CH), m("win_i").rearrange("p (k n) -> p k n", k=CH)
                for k in range(CH):
                    i = mm(out_[:, :], wxT[:, k, :], wi[:, k, :], start=(k == 0), stop=(k == CH - 1))
                i.then_inc(filled, 1)
                out_ = tile(("wxd",))
                for k in range(CH):
                    i = mm(out_[:, k * INNER:(k + 1) * INNER], m("wxpT")[:, k * P:(k + 1) * P], m("wdt"), start=True, stop=True)
                i.then_inc(filled, 1)
                pe.wait_ge(loaded["vec"], 16)
                out_ = tile(("bf",))
                for j in range(2 * CH):
                    for k in range(CH):
                        i = mm(out_[:, j:j + 1], wi[:, k, j * P:(j + 1) * P], v("b_x")[:, k:k + 1], start=(k == 0), stop=(k == CH - 1))
                i.then_inc(filled, 1)

            def front_conv(b):
                pe.wait_ge(loaded["x"], 16)
                wait_emptied(pe, ("wf",))
                for c in range(CH):
                    wait_bank_free(pe, ("xm", b, c))
                    mm(tile(("xm", b, c))[:, :], wf[:, c * P:(c + 1) * P], x[:, tok(b)], start=True, stop=True).then_inc(filled, 1)

            def front_gates(b):
                for c in range(CH):
                    wait_bank_free(pe, ("zm", b, c))
                    mm(tile(("zm", b, c))[:, :], wf[:, INNER + c * P:INNER + (c + 1) * P], x[:, tok(b)], start=True, stop=True).then_inc(filled, 1)
                wait_mats("win_z")
                for c in range(CH):
                    wait_bank_free(pe, ("z", b, c))
                    mm(tile(("z", b, c))[:, :], m("win_z")[:, c * P:(c + 1) * P], x[:, tok(b)], start=True, stop=True).then_inc(filled, 1)

            def front_delta(b):
                pe.wait_ge(xc_ready, b + 1)
                wait_emptied(pe, ("wxd",))
                for c in range(CH):
                    wait_bank_free(pe, ("dl", b, c))
                    for k in range(CH):
                        i = mm(tile(("dl", b, c))[:, :], wxd[:, k, c * P:(c + 1) * P], xc[b][:, k, :], start=(k == 0), stop=(k == CH - 1))
                    i.then_inc(filled, 1)
                wbc = m("wbc").rearrange("p (k n) -> p k n", k=CH)
                wait_bank_free(pe, ("bc", b))
                for k in range(CH):
                    i = mm(tile(("bc", b))[0:PARTS * BC, :], wbc[:, k, :], xc[b][:, k, :], start=(k == 0), stop=(k == CH - 1))
                i.then_inc(filled, 1)

            def scan(s):
                b, n = divmod(s, STATES)
                if s < BLOCKS * STATES:
                    if s == 0:
                        pe.wait_ge(small, 1)
                    if n == 0:
                        pe.wait_ge(split, 5 * (b + 1))
                    if s >= 2:
                        pe.wait_ge(in_ready, s - 1)
                    rows = PARTS * BC
                    mm(b_all[:, s % 2, :], selb[0:rows, n, :], parts[b][0:rows, :], start=True, stop=True).then_inc(b_ready, 1)
                    if s >= 1:
                        pe.wait_ge(c_copied, s)
                    mm(c_psum[:, :], selb[0:rows, STATES + n, :], parts[b][0:rows, :], start=True, stop=True).then_inc(c_ready, 1)
                if s >= LAG:
                    s -= LAG
                    b, n = divmod(s, STATES)
                    wait_product(pe, s)
                    if n == 0 and b > 0:
                        pe.wait_ge(y_out, 3 * b - 1)
                    for c in range(CH):
                        i = mm(y_sum[:, c, :], ident, state[s % RING][:, c, :], start=(n == 0), stop=(n == STATES - 1))
                    i.then_inc(summed, 1)

            def keys(b):
                pe.wait_ge(loaded["kv"], 16)
                wait_mats("wkT")
                wait_bank_free(pe, ("k", b))
                mm(tile(("k", b))[:, :], m("wkT"), kv[:, tok(b)], start=True, stop=True).then_inc(filled, 1)
                wait_bank_free(pe, ("ssk", b))
                wait_emptied(pe, ("k", b))
                for t in range(TILES):
                    i = mm(tile(("ssk", b))[:, t * HEADS:(t + 1) * HEADS], sq[:, t * P:(t + 1) * P], m("headsel"), start=True, stop=True)
                i.then_inc(filled, 1)

            def values(b):
                pe.wait_ge(loaded["bv"], 16)
                wait_bank_free(pe, ("v", b))
                for t in range(TILES):
                    o = tile(("v", b))[:, t * P:(t + 1) * P]
                    mm(o, kv[:, b * T + t * P:b * T + (t + 1) * P], m("wvT"), start=True, stop=False)
                    i = mm(o, ones[0:1, :], bv_row[0:1, :], start=False, stop=True)
                i.then_inc(filled, 1)

            def mamba_out(b):
                wait_mats("wouti")
                pe.wait_ge(y_out, 3 * (b + 1))
                w = m("wouti").rearrange("p (k n) -> p k n", k=CH)
                for c in range(CH):
                    wait_bank_free(pe, ("oi", b, c))
                    for k in range(CH):
                        i = mm(tile(("oi", b, c))[:, :], w[:, k, c * P:(c + 1) * P], xc[b][:, k, :], start=(k == 0), stop=(k == CH - 1))
                    i.then_inc(filled, 1)
                wait_bank_free(pe, ("oo", b))
                w = m("wouto").rearrange("p (k n) -> p k n", k=CH)
                for k in range(CH):
                    wait_emptied(pe, ("oi", b, k))
                    i = mm(tile(("oo", b))[:, :], w[:, k, :], gated[:, k, :], start=(k == 0), stop=(k == CH - 1))
                i.then_inc(filled, 1)

            def norm(b, i_):
                wait_bank_free(pe, ("mu", b, i_))
                if i_ == 1:
                    pe.wait_ge(res_ready, b + 1)
                else:
                    wait_emptied(pe, ("wo" if i_ == 2 else "w3", b))
                mm(tile(("mu", b, i_))[:, :], mean, y[:, :], start=True, stop=True).then_inc(filled, 1)
                wait_bank_free(pe, ("var", b, i_))
                pe.wait_ge(sq_ready, norm_index(b, i_) + 1)
                for t in range(TILES):
                    i = mm(tile(("var", b, i_))[:, t:t + 1], sq[:, t * P:(t + 1) * P], mean[:, 0:1], start=True, stop=True)
                i.then_inc(filled, 1)
                wait_bank_free(pe, ("rb", b, i_))
                pe.wait_ge(norm_dve, norm_steps(b, i_, 2))
                for t in range(TILES):
                    i = mm(tile(("rb", b, i_))[:, t * P:(t + 1) * P], ones, diag[:, t * P:(t + 1) * P], start=True, stop=True)
                i.then_inc(filled, 1)

            def query(b):
                wait_bank_free(pe, ("q", b))
                wait_emptied(pe, ("rb", b, 1))
                mm(tile(("q", b))[:, :], m("wqT"), x1[:, :], start=True, stop=True).then_inc(filled, 1)
                wait_bank_free(pe, ("ssq", b))
                wait_emptied(pe, ("q", b))
                for t in range(TILES):
                    i = mm(tile(("ssq", b))[:, t * HEADS:(t + 1) * HEADS], q2[:, t * P:(t + 1) * P], m("headsel"), start=True, stop=True)
                i.then_inc(filled, 1)
                wait_bank_free(pe, ("rqb", b))
                pe.wait_ge(rq_step, 2 * (b + 1))
                for t in range(TILES):
                    i = mm(tile(("rqb", b))[:, t * P:(t + 1) * P], rq_wide[:, t * P:(t + 1) * P], ident, start=True, stop=True)
                i.then_inc(filled, 1)

            def attend(b, p):
                if p < PAIRS:
                    if p == 0:
                        pe.wait_ge(qm_ready, HI * (b + 1))
                        pe.wait_ge(k_ready, b + 1)
                    for n in range(2):
                        wait_bank_free(pe, ("s", b, p, n))
                        for g in range(2):
                            for e in range(2):
                                t = (2 * p + e) * SEQ
                                i = mm(tile(("s", b, p, n))[e * SEQ:(e + 1) * SEQ, g * HI * SEQ:(g + 1) * HI * SEQ],
                                       kmask[:, 2 * n + g, t:t + SEQ], qmask[:, :, t:t + SEQ], start=True, stop=True)
                        i.then_inc(filled, 1)
                if p > 0:
                    p -= 1
                    wait_bank_free(pe, ("o", b, p))
                    if p == 0:
                        wait_emptied(pe, ("v", b))
                    for n in range(2):
                        wait_emptied(pe, ("s", b, p, n))
                    for e in range(2):
                        for i_ in range(HI):
                            for g in range(HG):
                                h = HI * g + i_
                                i = mm(tile(("o", b, p))[32 * g:32 * g + 32, e * SEQ:(e + 1) * SEQ],
                                       vmask[:, p, e, g, 32 * i_:32 * i_ + 32], attn[p % 2][:, h * SEQ:(h + 1) * SEQ],
                                       start=(i_ == 0), stop=(i_ == HI - 1), skip_group_check=True)
                    i.then_inc(filled, 1)

            def attn_out(b):
                wait_bank_free(pe, ("wo", b))
                wait_emptied(pe, ("o", b, PAIRS - 1))
                mm(tile(("wo", b))[:, :], m("woT"), heads_out, start=True, stop=True).then_inc(filled, 1)

            def gate_up(b, j):
                wait_mats("w1T")
                wait_emptied(pe, ("rb", b, 2))
                for key, w in (("w1", "w1T"), ("w2", "w2T")):
                    wait_bank_free(pe, (key, b, j))
                    mm(tile((key, b, j))[:, :], m(w)[:, j * P:(j + 1) * P], x2[:, :], start=True, stop=True).then_inc(filled, 1)

            def hid(key, w, src, before):
                w = m(w).rearrange("p (k n) -> p k n", k=FT)

                def part(b, j):
                    wait_bank_free(pe, (key, b, j))
                    for k in range(FT):
                        wait_emptied(pe, (before, b, k))
                        i = mm(tile((key, b, j))[:, :], w[:, k, j * P:(j + 1) * P], src[:, k, :], start=(k == 0), stop=(k == FT - 1))
                    i.then_inc(filled, 1)
                return part

            def down(b):
                wait_bank_free(pe, ("w3", b))
                w = m("w3T").rearrange("p (k n) -> p k n", k=FT)
                for k in range(FT):
                    wait_emptied(pe, ("h2", b, k))
                    i = mm(tile(("w3", b))[:, :], w[:, k, :], hid_c[:, k, :], start=(k == 0), stop=(k == FT - 1))
                i.then_inc(filled, 1)

            parts_of = {"prep": prep, "front_conv": front_conv, "front_gates": front_gates, "front_delta": front_delta,
                        "scan": scan, "keys": keys, "values": values, "mamba_out": mamba_out, "norm": norm, "query": query,
                        "attend": attend, "attn_out": attn_out, "gate_up": gate_up,
                        "hid1": hid("h1", "h1T", hid_a, "w2"), "hid2": hid("h2", "h2T", hid_b, "h1"), "down": down}
            for kind, *at in steps:
                if kind in parts_of:
                    parts_of[kind](*at)

        @block.scalar
        def _(act):
            act_ = nc.scalar.activation

            def prep():
                act.wait_ge(loaded["vec"], 16)
                act_(neg_a[:, :], v("a_log"), ACT.Exp).then_inc(a_exp, 1)
                wait_filled(act, ("wf",))
                act_(wf[:, :], tile(("wf",))[:, :], ACT.Copy).then_inc(used["act"], 1)
                wait_filled(act, ("wxd",))
                act_(wxd[:, :, :].rearrange("p k n -> p (k n)"), tile(("wxd",))[:, :], ACT.Copy).then_inc(used["act"], 1)

            def front_conv(b):
                if b == 0:
                    wait_emptied(act, ("bf",))
                    act.wait_ge(zeroed, 1)
                else:
                    act.wait_ge(conv_step, CH * TAPS * b)
                for c in range(CH):
                    wait_filled(act, ("xm", b, c))
                    act_(xpad[:, c, :, TAPS - 1:], tile(("xm", b, c))[:, :].rearrange("p (s t) -> p s t", t=SEQ),
                         ACT.Identity, bias=bf[:, c:c + 1]).then_inc(used["act"], 1)

            def front_gates(b):
                act.wait_ge(small, 2)
                for c in range(CH):
                    wait_filled(act, ("zm", b, c))
                    act_(mgate[b][:, c, :], tile(("zm", b, c))[:, :], ACT.Silu, bias=bf[:, CH + c:CH + c + 1]).then_inc(used["act"], 1)
                for c in range(CH):
                    wait_filled(act, ("z", b, c))
                    act_(zgate[b][:, c, :], tile(("z", b, c))[:, :], ACT.Tanh, bias=hbz[:, c:c + 1], scale=0.5).then_inc(used["act"], 1)

            def front_delta(b):
                act.wait_ge(conv_step, CH * TAPS * (b + 1))
                act_(xc[b][:, :, :], conv, ACT.Silu).then_inc(xc_ready, 1)
                if b > 0:
                    act.wait_ge(soft_dve, 5 * b)
                for c in range(CH):
                    wait_filled(act, ("dl", b, c))
                    act_(pre[:, c, :], tile(("dl", b, c))[:, :], ACT.Identity, bias=v("b_dt")[:, c:c + 1]).then_inc(used["act"], 1)
                wait_emptied(act, ("dl", b, CH - 1))
                act_(expo, pre, ACT.Abs).then_inc(soft_act, 1)
                act.wait_ge(soft_act, 3 * b + 1)
                act_(expo, expo, ACT.Exp, scale=-1.0).then_inc(soft_act, 1)
                act.wait_ge(soft_act, 3 * b + 2)
                act_(logt, expo, ACT.Ln, bias=1.0).then_inc(soft_act, 1)

            def scan(s):
                if s >= BLOCKS * STATES:
                    return
                b, n = divmod(s, STATES)
                if s == 0:
                    act.wait_ge(small, 3)
                    act.wait_ge(zeroed, 2)
                if n == 0:
                    act.wait_ge(soft_dve, 5 * b + 4)
                if s >= DA_RING:
                    act.wait_ge(scanned, s - DA_RING + 1)
                for c in range(CH):
                    act_(decay[s % DA_RING][:, c, :].rearrange("p (s t) -> p s t", t=SEQ)[:, :, 1:],
                         delta[b][:, c, :].rearrange("p (s t) -> p s t", t=SEQ)[:, :, 1:],
                         ACT.Exp, scale=neg_a[:, c * STATES + n:c * STATES + n + 1]).then_inc(decay_ready, 1)
                act.wait_ge(c_ready, s + 1)
                if s >= CS_RING:
                    wait_product(act, s - CS_RING)
                act_(c_all[s % CS_RING][:, :], c_psum[:, :], ACT.Copy).then_inc(c_copied, 1)

            def keys(b):
                if b == 0:
                    act.wait_ge(zeroed, 4)
                wait_filled(act, ("k", b))
                for g in range(HG):
                    r = slice(32 * g, 32 * g + 32)
                    i = act_(kmask[r, g, :], tile(("k", b))[r, :], ACT.Identity, bias=v("bk")[r, :])
                i.then_inc(k_ready, 1)
                act_(sq[:, :], tile(("k", b))[:, :], ACT.Square, bias=v("bk")).then_inc(used["act"], 1)

            def norm(b, i):
                wait_emptied(act, ("mu", b, i))
                act_(sq[:, :], dev[:, :], ACT.Square).then_inc(sq_ready, 1)
                wait_filled(act, ("var", b, i))
                act_(std[:, :], tile(("var", b, i))[:, 0:TILES], ACT.Sqrt, bias=v("eps")).then_inc(used["act"], 1)

            def query(b):
                wait_filled(act, ("q", b))
                act_(q, tile(("q", b))[:, :], ACT.Identity, bias=v("bq")).then_inc(q_ready, 1)
                act_(q2, tile(("q", b))[:, :], ACT.Square, bias=v("bq")).then_inc(used["act"], 1)
                wait_filled(act, ("rqb", b))
                act_(rq_all, tile(("rqb", b))[:, :], ACT.Copy).then_inc(used["act"], 1)

            def attend(b, p):
                if p == PAIRS:
                    return
                for n in range(2):
                    wait_filled(act, ("s", b, p, n))
                    if p >= 2:
                        wait_filled(act, ("o", b, p - 2))
                    act_(attn[p % 2][:, n * T:(n + 1) * T], tile(("s", b, p, n))[:, :], ACT.Square).then_inc(used["act"], 1)

            def gate_up(b, j):
                wait_filled(act, ("w1", b, j))
                if j > 0:
                    wait_emptied(act, ("w2", b, j - 1))
                act_(up[:, :], tile(("w1", b, j))[:, :], ACT.Silu, scale=v("s1")[:, j:j + 1]).then_inc(used["act"], 1)

            def hid1(b, j):
                wait_filled(act, ("h1", b, j))
                act_(hid_b[:, j, :], tile(("h1", b, j))[:, :], ACT.Gelu, scale=v("h1s")[:, j:j + 1]).then_inc(used["act"], 1)

            def hid2(b, j):
                wait_filled(act, ("h2", b, j))
                act_(hid_c[:, j, :], tile(("h2", b, j))[:, :], ACT.Gelu, scale=v("h2s")[:, j:j + 1]).then_inc(used["act"], 1)

            parts_of = {"prep": prep, "front_conv": front_conv, "front_gates": front_gates, "front_delta": front_delta,
                        "scan": scan, "keys": keys, "norm": norm, "query": query, "attend": attend, "gate_up": gate_up,
                        "hid1": hid1, "hid2": hid2}
            for kind, *at in steps:
                if kind in parts_of:
                    parts_of[kind](*at)

        @block.vector
        def _(dve):
            vec_ = nc.vector

            def prep():
                dve.wait_ge(loaded["vec"], 16)
                rows = PARTS * BC
                vec_.tensor_copy(selb[0:rows, :, :], v("sel")[0:rows, :, None].broadcast_to([rows, BC, P])).then_inc(small, 1)
                vec_.tensor_scalar(hbz[:, :], v("b_z"), 0.5, None, ALU.mult).then_inc(small, 1)
                dve.wait_ge(a_exp, 1)
                vec_.tensor_scalar(neg_a[:, :], neg_a[:, :], -1.0, None, ALU.mult).then_inc(small, 1)
                wait_filled(dve, ("bf",))
                vec_.tensor_copy(bf[:, :], tile(("bf",))[:, 0:2 * CH]).then_inc(used["dve"], 1)

            def front_conv(b):
                cv = conv.rearrange("p c (s t) -> p c s t", t=SEQ)
                for c in range(CH):
                    wait_emptied(dve, ("xm", b, c))
                    w = v("conv_w")[:, c * TAPS:(c + 1) * TAPS]
                    if b > 0 and c == 0:
                        dve.wait_ge(xc_ready, b)
                    vec_.tensor_scalar(cv[:, c], xpad[:, c, :, TAPS - 1:], w[:, TAPS - 1:TAPS], v("conv_b")[:, c:c + 1],
                                       ALU.mult, ALU.add).then_inc(conv_step, 1)
                    for k in range(TAPS - 1):
                        dve.wait_ge(conv_step, (b * CH + c) * TAPS + k + 1)
                        vec_.scalar_tensor_tensor(out=cv[:, c], in0=xpad[:, c, :, k:k + SEQ], scalar=w[:, k:k + 1], in1=cv[:, c],
                                                  op0=ALU.mult, op1=ALU.add).then_inc(conv_step, 1)

            def front_delta(b):
                wait_filled(dve, ("bc", b))
                bc = tile(("bc", b))
                r3, r2 = slice(0, PARTS * BC), slice(2 * BC, 3 * BC)
                vec_.tensor_copy(parts[b][r3, :], bc[r3, :]).then_inc(split, 1)
                dve.wait_ge(split, 5 * b + 1)
                vec_.tensor_tensor(rest[r3, :], bc[r3, :], parts[b][r3, :], ALU.subtract).then_inc(used["dve"], 1)
                wait_emptied(dve, ("bc", b))
                vec_.tensor_copy(mid[r3, :], rest[r3, :]).then_inc(split, 1)
                dve.wait_ge(split, 5 * b + 2)
                vec_.tensor_copy(parts[b][BC:2 * BC, :], mid[BC:2 * BC, :]).then_inc(split, 1)
                vec_.tensor_tensor(rest[r2, :], rest[r2, :], mid[r2, :], ALU.subtract).then_inc(split, 1)
                dve.wait_ge(split, 5 * b + 4)
                vec_.tensor_copy(parts[b][r2, :], rest[r2, :]).then_inc(split, 1)
                dve.wait_ge(soft_act, 3 * b + 2)
                vec_.tensor_scalar(trunc, expo, 1.0, -1.0, ALU.add, ALU.add).then_inc(soft_dve, 1)
                dve.wait_ge(soft_dve, 5 * b + 1)
                vec_.tensor_tensor(trunc, expo, trunc, ALU.subtract).then_inc(soft_dve, 1)
                dve.wait_ge(soft_act, 3 * b + 3)
                vec_.scalar_tensor_tensor(out=logt, in0=pre, scalar=0.0, in1=logt, op0=ALU.max, op1=ALU.add).then_inc(soft_dve, 1)
                dve.wait_ge(soft_dve, 5 * b + 3)
                vec_.tensor_tensor(delta[b][:, :, :], logt, trunc, ALU.add).then_inc(soft_dve, 1)
                dve.wait_ge(soft_dve, 5 * b + 4)
                vec_.tensor_tensor(du[b][:, :, :], delta[b][:, :, :], xc[b][:, :, :], ALU.mult).then_inc(soft_dve, 1)

            def scan(s):
                if s < BLOCKS * STATES:
                    b, n = divmod(s, STATES)
                    if n == 0:
                        dve.wait_ge(soft_dve, 5 * (b + 1))
                    dve.wait_ge(b_ready, s + 1)
                    if s >= RING:
                        dve.wait_ge(summed, s - RING + 1)
                    vec_.tensor_tensor(state[s % RING][:, :, :], du[b][:, :, :],
                                       b_all[:, s % 2, None, :].broadcast_to([P, CH, T]), ALU.mult).then_inc(in_ready, 1)
                if 1 <= s <= BLOCKS * STATES:
                    s1 = s - 1
                    dve.wait_ge(decay_ready, CH * (s1 + 1))
                    dve.wait_ge(in_ready, s1 + 1)
                    h = state[s1 % RING][:, :, :].rearrange("p c t -> p (c t)")
                    vec_.tensor_tensor_scan(h, decay[s1 % DA_RING][:, :, :].rearrange("p c t -> p (c t)"), h, 0.0,
                                            ALU.mult, ALU.add).then_inc(scanned, 1)
                if 2 <= s <= BLOCKS * STATES + 1 and (s - 2) % STATES not in POOL_STATES:
                    output_product(dve, vec_, s - 2, hc_dve)

            def output_product(eng, engine, s, done):
                eng.wait_ge(scanned, s + 1)
                eng.wait_ge(c_copied, s + 1)
                h = state[s % RING][:, :, :]
                engine.tensor_tensor(h, h, c_all[s % CS_RING][:, None, :].broadcast_to([P, CH, T]), ALU.mult).then_inc(done, 1)

            def keys(b):
                wait_filled(dve, ("ssk", b))
                vec_.tensor_scalar(ssk[:, :, :].rearrange("p t h -> p (t h)"), tile(("ssk", b))[:, 0:TILES * HEADS], L2_EPS, None,
                                   ALU.add).then_inc(used["dve"], 1)
                wait_emptied(dve, ("ssk", b))
                vec_.reciprocal(rk[:, :, :], ssk[:, :, :]).then_inc(rk_ready, 1)

            def values(b):
                wait_filled(dve, ("v", b))
                dve.wait_ge(rk_ready, b + 1)
                if b == 0:
                    dve.wait_ge(zeroed, 3)
                for p in range(PAIRS):
                    for e in range(2):
                        r = slice(e * SEQ, (e + 1) * SEQ)
                        src = tile(("v", b))[r, p * P:(p + 1) * P].rearrange("p (g i d) -> p g i d", g=HG, i=HI)
                        dst = vmask[r, p, e, :, :].rearrange("p g (i w) -> p g i w", i=HI)[:, :, :, 0:DK]
                        scale = rk[r, p, :].rearrange("p (g i) -> p g i", g=HG)[:, :, :, None].broadcast_to([SEQ, HG, HI, DK])
                        i = vec_.tensor_tensor(dst, src, scale, ALU.mult)
                i.then_inc(used["dve"], 1)

            def mamba_out(b):
                dve.wait_ge(summed, STATES * (b + 1))
                for c in range(CH):
                    vec_.scalar_tensor_tensor(out=du[b][:, c, :], in0=xc[b][:, c, :], scalar=v("d_skip")[:, c:c + 1],
                                              in1=y_sum[:, c, :], op0=ALU.mult, op1=ALU.add).then_inc(y_out, 1)
                dve.wait_ge(y_out, 3 * b + 2)
                vec_.tensor_tensor(xc[b][:, :, :], du[b][:, :, :], mgate[b][:, :, :], ALU.mult).then_inc(y_out, 1)
                for c in range(CH):
                    wait_filled(dve, ("oi", b, c))
                    vec_.scalar_tensor_tensor(out=gated[:, c, :], in0=zgate[b][:, c, :], scalar=1.0, in1=tile(("oi", b, c))[:, :],
                                              op0=ALU.add, op1=ALU.mult).then_inc(used["dve"], 1)
                wait_filled(dve, ("oo", b))
                vec_.scalar_tensor_tensor(out=dev[:, :], in0=tile(("oo", b))[:, :], scalar=0.5, in1=x[:, tok(b)],
                                          op0=ALU.mult, op1=ALU.add).then_inc(used["dve"], 1)
                wait_emptied(dve, ("oo", b))
                vec_.tensor_scalar(y[:, :], dev[:, :], v("b_out"), None, ALU.add).then_inc(res_ready, 1)

            def norm(b, i):
                wait_filled(dve, ("mu", b, i))
                vec_.tensor_tensor(dev[:, :], y[:, :], tile(("mu", b, i))[:, :], ALU.subtract).then_inc(used["dve"], 1)
                wait_emptied(dve, ("var", b, i))
                vec_.reciprocal(rstd[:, :], std[:, :]).then_inc(norm_dve, 1)
                dve.wait_ge(norm_dve, norm_steps(b, i, 1))
                for t in range(TILES):
                    ins = vec_.tensor_scalar(diag[:, t * P:(t + 1) * P], ident, rstd[:, t:t + 1], None, ALU.mult)
                ins.then_inc(norm_dve, 1)
                wait_filled(dve, ("rb", b, i))
                if i == 1 and b > 0:
                    dve.wait_ge(stored, 16 * b)
                vec_.tensor_tensor({1: x1, 2: x2, 3: final}[i][:, :], dev[:, :], tile(("rb", b, i))[:, :],
                                   ALU.mult).then_inc(used["dve"], 1)

            def query(b):
                dve.wait_ge(q_ready, b + 1)
                for i in range(HI):
                    vec_.tensor_scalar(qmask[:, i, :], q, v("hmask")[:, i:i + 1], None, ALU.mult).then_inc(qm_ready, 1)
                wait_filled(dve, ("ssq", b))
                vec_.tensor_scalar(ssq[:, :, :].rearrange("p t h -> p (t h)"), tile(("ssq", b))[:, 0:TILES * HEADS], L2_EPS, None,
                                   ALU.add).then_inc(used["dve"], 1)
                wait_emptied(dve, ("ssq", b))
                vec_.reciprocal(rq[:, :, :], ssq[:, :, :]).then_inc(rq_step, 1)
                dve.wait_ge(rq_step, 2 * b + 1)
                vec_.tensor_copy(rq_wide.rearrange("p (t h d) -> p t h d", h=HEADS, d=DK),
                                 rq[:, :, :, None].broadcast_to([P, TILES, HEADS, DK])).then_inc(rq_step, 1)

            def attend(b, p):
                if p == 0:
                    return
                p -= 1
                wait_filled(dve, ("o", b, p))
                wait_emptied(dve, ("rqb", b))
                vec_.tensor_tensor(heads_out[:, p * P:(p + 1) * P], tile(("o", b, p))[:, 0:P], rq_all[:, p * P:(p + 1) * P],
                                   ALU.mult).then_inc(used["dve"], 1)

            def attn_out(b):
                wait_filled(dve, ("wo", b))
                vec_.scalar_tensor_tensor(out=y[:, :], in0=tile(("wo", b))[:, :], scalar=v("bo"), in1=x1[:, :],
                                          op0=ALU.add, op1=ALU.add).then_inc(used["dve"], 1)

            def gate_up(b, j):
                wait_filled(dve, ("w2", b, j))
                wait_emptied(dve, ("w1", b, j))
                vec_.scalar_tensor_tensor(out=hid_a[:, j, :], in0=tile(("w2", b, j))[:, :], scalar=v("s2")[:, j:j + 1], in1=up[:, :],
                                          op0=ALU.mult, op1=ALU.mult).then_inc(used["dve"], 1)

            def down(b):
                wait_filled(dve, ("w3", b))
                vec_.scalar_tensor_tensor(out=y[:, :], in0=tile(("w3", b))[:, :], scalar=v("s3"), in1=x2[:, :],
                                          op0=ALU.mult, op1=ALU.add).then_inc(used["dve"], 1)

            parts_of = {"prep": prep, "front_conv": front_conv, "front_delta": front_delta, "scan": scan, "keys": keys,
                        "values": values, "mamba_out": mamba_out, "norm": norm, "query": query, "attend": attend,
                        "attn_out": attn_out, "gate_up": gate_up, "down": down}
            for kind, *at in steps:
                if kind in parts_of:
                    parts_of[kind](*at)

        @block.gpsimd
        def _(pool):
            nc.gpsimd.memset(xpad[:, :, :, :], 0.0).then_inc(zeroed, 1)
            for d in decay:
                i = nc.gpsimd.memset(d[:, :, :], 0.0)
            i.then_inc(zeroed, 1)
            nc.gpsimd.memset(vmask[:, :, :, :, :], 0.0).then_inc(zeroed, 1)
            nc.gpsimd.memset(kmask[:, :, :], 0.0).then_inc(zeroed, 1)
            for s in range(BLOCKS * STATES):
                if s % STATES in POOL_STATES:
                    pool.wait_ge(scanned, s + 1)
                    pool.wait_ge(c_copied, s + 1)
                    h = state[s % RING][:, :, :]
                    nc.gpsimd.tensor_tensor(h, h, c_all[s % CS_RING][:, None, :].broadcast_to([P, CH, T]),
                                            ALU.mult).then_inc(hc_pool, 1)


def kernel(**inputs):
    import concourse.bacc as bacc
    from concourse.bass_utils import run_bass_kernel_spmd

    a = {k.replace("L0_", ""): np.asarray(v) for k, v in inputs.items()}

    def rows(w):
        return np.reshape(w, (-1, P, w.shape[1])).transpose(1, 0, 2).reshape(P, -1)

    def col(w):
        return np.reshape(w, (-1, P)).T

    f = np.float32
    heads = np.arange(P) // DK
    parts = {
        "win_xT": rows(a["attn_W_in_o"][:, :INNER].T), "win_z": a["attn_W_in_o"][:, INNER:],
        "win_i": rows(a["attn_W_in_i"]), "wxpT": a["attn_W_xp"][:, :P].T, "wdt": a["attn_W_dt"],
        "wbc": rows(np.concatenate([a["attn_W_xp"][:, P:]] * PARTS, 1)),
        "ident": np.eye(P, dtype=f), "mean": np.full((P, P), 1 / P, f), "ones": np.ones((P, P), f),
        "headsel": (heads[:, None] == np.arange(HEADS)).astype(f),
        "wkT": a["xattn_Wk_w"].T, "wvT": a["xattn_Wv_w"].T, "wqT": a["xattn_Wq_w"].T, "woT": a["xattn_Wo_w"].T,
        "wouti": rows(a["attn_W_out_i"]), "wouto": rows(a["attn_W_out_o"]),
        "w1T": a["ffn_w1_w"].T, "w2T": a["ffn_w2_w"].T, "h1T": rows(a["ffn_h1_w"].T), "h2T": rows(a["ffn_h2_w"].T),
        "w3T": rows(a["ffn_w3_w"].T)}
    vectors = {
        "b_x": col(a["attn_b_in_o"][:INNER]), "b_z": col(a["attn_b_in_o"][INNER:]),
        "conv_w": rows(a["attn_conv_w"]), "conv_b": col(a["attn_conv_b"]), "b_dt": col(a["attn_b_dt"]),
        "a_log": rows(a["attn_A_log"]), "d_skip": col(a["attn_D_skip"]), "b_out": col(a["attn_b_out_o"]),
        "bq": col(a["xattn_Wq_b"]), "bk": col(a["xattn_Wk_b"]), "bo": col(a["xattn_Wo_b"]),
        "s1": col(a["ffn_w1_s"]), "s2": col(a["ffn_w2_s"]), "h1s": col(a["ffn_h1_s"]), "h2s": col(a["ffn_h2_s"]),
        "s3": col(a["ffn_w3_s"]), "hmask": (heads[:, None] % HI == np.arange(HI)).astype(f),
        "eps": np.full((P, 1), LN_EPS, f), "sel": (np.arange(P)[:, None] % BC == np.arange(BC)).astype(f)}
    arrays = {
        "xT": np.ascontiguousarray(a["x"].reshape(TOKENS, P).T),
        "ctxT": np.ascontiguousarray(a["ctx_1024"].reshape(TOKENS, P).T),
        "mats": np.ascontiguousarray(np.concatenate([parts[n] for n, _ in MATS], 1)),
        "vecs": np.ascontiguousarray(np.concatenate([vectors[n] for n, _ in VECS], 1)),
        "bv": np.ascontiguousarray(a["xattn_Wv_b"].reshape(1, P))}
    nc = bacc.Bacc("TRN2", target_bir_lowering=False, num_devices=1)
    args = [nc.dram_tensor(n, list(v.shape), mybir.dt.from_np(v.dtype), kind="ExternalInput").ap() for n, v in arrays.items()]
    out = nc.dram_tensor("outT", [P, TOKENS], F32, kind="ExternalOutput").ap()
    decoder_layer(nc, *args, out)
    r = run_bass_kernel_spmd(nc, [arrays], core_ids=[0])
    return r.results[0]["outT"].T.reshape(BATCH, SEQ, P)
```

```python
from contextlib import ExitStack

import concourse.bass as bass
from concourse import mybir
import numpy as np

ALU = mybir.AluOpType
AX = mybir.AxisListType
ACT = mybir.ActivationFunctionType
F32 = mybir.dt.float32
BF16 = mybir.dt.bfloat16
I32 = mybir.dt.int32

P = 128
BATCH, SEQ = 16, 64
TOKENS = BATCH * SEQ
BLOCKS = 4
T = TOKENS // BLOCKS
SEQS = T // SEQ
PAIRS = SEQS // 2
TILES = T // P
INNER = 256
CH = INNER // P
STATES = 16
SG = 2
STEPS = STATES // SG
TAPS = 4
HEADS, DK = 16, 8
HG, HI = 4, 4
HID = 512
FT = HID // P
VROW = HI * (32 + DK)
PARTS = 3
BC = 2 * STATES
WORK_BANKS = 4
RING = 4
DA_RING = 2
Y_STEPS = CH + 2
WARM_UP = 18
KEEP = 2

MATS = [("win_xT", CH * P), ("win_i", CH * 2 * INNER), ("wxpT", INNER), ("wdt", INNER), ("win_z", INNER),
        ("wbc", CH * PARTS * BC), ("ident", P), ("mean", P), ("centre", P), ("ones", P), ("headsel", HEADS),
        ("wkT", P), ("wvT", P), ("wouto", CH * P), ("wo", P), ("w3", FT * P), ("wouti", CH * INNER), ("wqT", P),
        ("w1T", HID), ("w2T", HID), ("h1T", FT * HID), ("h2T", FT * HID)]
VECS = [("b_x", CH), ("b_z", CH), ("conv_w", CH * TAPS), ("conv_b", CH), ("b_dt", CH), ("a_log", CH * STATES),
        ("d_skip", CH), ("b_out_bo", 2), ("bq", 1), ("bk", 1), ("s1", FT), ("s2", FT), ("h1s", FT),
        ("h2s", FT), ("s3", 1), ("hmask", HI), ("sel", BC)]
LN_EPS, L2_EPS = 1e-5, 1e-8
ROUNDS = 3
ROOT_GUESS = 0x5F3759DF


def columns(parts):
    at, n = {}, 0
    for name, w in parts:
        at[name] = (n, n + w)
        n += w
    return at, n


MAT_AT, MAT_COLS = columns(MATS)
VEC_AT, VEC_COLS = columns(VECS)
LOADS = [("win_xT", "win_i"), ("wxpT", "wbc"), ("ident", "headsel"), ("wkT", "wvT"), ("wouto", "w3"), ("wouti", "wqT"), ("w1T", "h2T")]



NAMES = {
 "front": ("xm", "conv", "xc", "delta", "bc", "soft", "soft_end"),
 "gates": ("gate_m", "gate_z"),
 "kv": ("keys", "key_norm", "values"),
 "attn": ("mamba_y", "gate_out", "proj_out", "norm_var1", "norm_scale1", "norm_apply1", "query", "query_norm", "query_back", "attend0", "attend1", "attend2", "attn_out", "norm_var2", "norm_scale2", "norm_apply2"),
 "ffn": ("gate_up0","gate_up1","gate_up2","gate_up3","hid10","hid11","hid12","hid13","hid20","hid21","hid22","hid23","down","norm_var3","norm_scale3","norm_apply3")}

LAG_OF = [("act", k) for k in ("xm", "xc", "delta", "bc", "soft", "gate_m", "gate_z", "keys", "scan_in", "scan_c", "norm_var", "query", "query_back", "attend", "gate_up", "hid1", "hid2")] + [
  ("dve", k) for k in ("conv", "delta", "bc", "soft", "soft_end", "key_norm", "values", "scan_in", "scan", "scan_out", "mamba_y", "gate_out", "proj_out", "norm_var", "norm_scale", "norm_apply", "query", "query_norm", "attend", "attn_out", "gate_up", "down")] + [("pool", "soft"), ("pool", "scan_out")]

def build_schedule(lanes):
    places = []
    def put(at, *name):
        places.append((at, len(places), name))
    def step(n, b):
        if n[-1].isdigit() and n[:-1] in ("norm_var","norm_scale","norm_apply","attend","gate_up","hid1","hid2"):
            return (n[:-1], b, int(n[-1]))
        return (n, b)
    put(-20, "prep")
    put(lanes["prep2"][0], "prep2")
    for name, lag in zip(("scan_in", "scan_c", "scan", "scan_out"), lanes["scan"]):
        for s in range(BLOCKS * STEPS): put(s + lag, name, s)
    put(lanes["centre"][0], "centre_x")
    put(lanes["centre"][1], "centre_w")
    for b in range(BLOCKS):
        for k, ns in NAMES.items():
            f = lanes[f"{k}{b}" if f"{k}{b}" in lanes else k]
            for n, at in zip(ns, f): put(at + STEPS * b, *step(n, b))
    lag = dict(zip(LAG_OF, lanes["lag"]))
    return {engine: [name for _, _, name in sorted((at + lag.get((engine, name[0]), 0), i, name) for at, i, name in places)]
            for engine in ("pe", "act", "dve", "pool")}
def lin(a,z,n): return [round((a+(z-a)*i/n)*4)/4 for i in range(n)]
LANES = {"front0": [-14.25, -14.0, -14.0, -5.5, -4.25, -2.5, -2.5], "front1": [-9.0, -8.5, -7.25, -7.0, -5.75, -4.25, -3.0], "front": [-5.5, -4.5, -2.75, -2, -1.5, -0.5, -0.5], "gates0": [-6.0, -6.0], "gates1": [-7.0, -5.75], "gates": [-3.0, -3.0], "kv": [11.25, 11.5, 12.25], "kv0": [6.5, 6.5, 7.0], "kv1": [2.75, 2.75, 6.0], "attn": [10.25, 11.5, 11.75, 12.25, 12.75, 13.5, 14.0, 14.5, 15.0, 15.0, 15.25, 15.75, 16.5, 17.0, 17.0, 17.75], "attn3": [9.75, 10.75, 11.25, 12.25, 12.75, 13.25, 13.25, 14.5, 15.25, 15.25, 15.25, 15.25, 15.75, 16.0, 16.0, 16.75], "ffn": [18.5, 19.25, 19.75, 20.0, 21.25, 21.25, 21.5, 21.5, 22.0, 22.0, 22.5, 24.5, 25.0, 25.25, 25.75, 26.0], "ffn2": [18.25, 19.5, 20.0, 20.25, 20.5, 20.5, 21.75, 23.25, 23.75, 24.25, 24.5, 24.75, 25.25, 27.5, 28.0, 32.25], "ffn3": [17.0, 17.0, 17.25, 17.25, 19.0, 19.0, 20.0, 20.0, 20.0, 20.0, 24.25, 24.5, 30.25, 30.25, 30.25, 30.5], "centre": [1.0, -0.25], "prep2": [-11.0], "scan": [0, 1, 1, 1.75], "lag": [0.0, 0.0, 0.0, 0.0, 0.0, 0.0, 0.0, -0.25, 0.0, 0.0, 0.0, 0.0, 0.0, 0.25, 0.0, 0.0, 0.0, 0.0, 0.25, 0.0, 0.0, 0.0, -0.25, 0.0, 0.0, 0.0, 0.0, 0.0, 0.0, 0.0, 0.0, 0.0, 0.0, 0.0, 0.0, 0.0, 0.0, 0.0, 0.0, -0.25, 0.0]}
def schedule(): return build_schedule(LANES)

def work_tiles(step):
    kind, *at = step
    b = at[0] if at else 0
    if kind == "prep":
        return [(("wf",), "act"), (("bf",), "dve")]
    if kind == "prep2":
        return [(("bfm",), "dve"), (("wxd",), "act")]
    if kind == "centre_w":
        return [(("wc",), "act"), (("w3c",), "act")]
    if kind == "centre_x":
        return [(("bias",), "dve")] + [(("xcen", n), "dve") for n in range(TOKENS // 512)]
    if kind == "attend":
        p = at[1]
        return [(("s", b, p, n), "act") for n in range(2) if p < PAIRS] + [(("o", b, p - 1), "dve")] * (p > 0)
    tiles = {"xm": [("xm", "act")], "gate_m": [("zm", "act")], "gate_z": [("z", "act")],
             "delta": [("dl", "dve")], "bc": [("bc", "dve")], "keys": [("k", "act")], "key_norm": [("ssk", "dve")],
             "values": [("v", "dve")], "gate_out": [("oi", "dve")], "proj_out": [("oo", "dve")],
             "norm_var": [("var", "dve")], "norm_apply": [("rb", "dve")], "query": [("q", "act")],
             "query_norm": [("ssq", "dve")], "query_back": [("rqb", "act")], "attn_out": [("wo", "dve")],
             "gate_up": [("gu", "dve")], "hid1": [("h1", "act")], "hid2": [("h2", "act")], "down": [("w3", "dve")]}
    return [((name, *at), engine) for name, engine in tiles.get(kind, [])]


def decoder_layer(nc, xT, ctxT, mats, vecs, bv, out):
    steps = schedule()
    work = [w for step in steps["pe"] for w in work_tiles(step)]
    number = {key: n for n, (key, _) in enumerate(work)}
    emptied = {}
    for engine in ("act", "dve"):
        keys_of = [key for step in steps[engine] for key, by in work_tiles(step) if by == engine]
        emptied.update((key, n + 1) for n, key in enumerate(keys_of))

    with ExitStack() as ctx:
        def sb(name, shape, dt=F32):
            return ctx.enter_context(nc.sbuf_tensor(name, [P, *shape], dt))

        def psum(name, shape):
            return ctx.enter_context(nc.psum_tensor(name, [P, *shape], F32))

        def sem(name):
            return ctx.enter_context(nc.semaphore(name))

        mat = sb("mat", [MAT_COLS])
        vec = sb("vec", [VEC_COLS])
        bv_row = sb("bv_row", [P])
        s3_centre = sb("s3_centre", [P])
        x = sb("x", [TOKENS])
        kv = sb("kv", [TOKENS])
        wf = sb("wf", [2 * INNER])
        wxd = sb("wxd", [CH, INNER])
        bf = sb("bf", [2 * CH])
        hbz = sb("hbz", [CH])
        neg_a = sb("neg_a", [CH * STATES])
        selb = sb("selb", [BC], BF16)
        xpad = sb("xpad", [CH, SEQS, TAPS - 1 + SEQ])
        xc, zgate, mgate, delta, du = ([sb(f"{n}{b}", [CH, T]) for b in range(KEEP)]
                                       for n in ("xc", "zgate", "mgate", "delta", "du"))
        parts = [sb(f"parts{b}", [T], BF16) for b in range(KEEP)]
        mid = sb("mid", [T], BF16)
        decay = [sb(f"decay{i}", [SG, CH, T]) for i in range(DA_RING)]
        state = [sb(f"state{i}", [SG, CH, T]) for i in range(RING)]
        c_all = [sb(f"c_all{i}", [SG, T]) for i in range(2)]
        acc = [sb(f"acc{i}", [SG, CH, T]) for i in range(2)]
        kmask = [sb(f"kmask{b}", [HG, T]) for b in range(KEEP)]
        vmask = [sb(f"vmask{b}", [PAIRS, 2, HG, VROW]) for b in range(KEEP)]
        warm = sb("warm", [BLOCKS])
        ssk, rk, ssq, rq = (sb(n, [TILES, HEADS]) for n in ("ssk", "rk", "ssq", "rq"))
        x_centred = sb("x_centred", [TOKENS])
        b_centred = sb("b_centred", [2])
        wouto_wo_c = sb("wouto_wo_c", [CH + 1, P])
        w3_c = sb("w3_c", [FT, P])
        conv, pre, expo, logt, trunc, gated = (sb(n, [CH, T]) for n in ("conv", "pre", "expo", "logt", "trunc", "gated"))
        hid_a, hid_b, hid_c = (sb(n, [FT, T]) for n in ("hid_a", "hid_b", "hid_c"))
        qmask = sb("qmask", [HI, T])
        up = [sb(f"up{i}", [T]) for i in range(2)]
        half_s1, half_s12 = sb("half_s1", [FT]), sb("half_s12", [FT])
        dev, sq, diag = ({k: sb(f"{n}_{k}", [T]) for k in ("attn", "ffn")} for n in ("dev", "sq", "diag"))
        var, root, newton = ({k: sb(f"{n}_{k}", [TILES]) for k in ("attn", "ffn")} for n in ("var", "root", "newton"))
        k2, x1, q, q2, heads_out, rq_all, rq_wide = (sb(n, [T]) for n in ("k2", "x1", "q", "q2", "heads_out", "rq_all", "rq_wide"))
        x2 = [sb(f"x2_{i}", [T]) for i in range(2)]
        final = [sb(f"final{i}", [T]) for i in range(2)]
        bc_rest = sb("bc_rest", [T])

        def m(name):
            return mat[:, MAT_AT[name][0]:MAT_AT[name][1]]

        def v(name):
            return vec[:, VEC_AT[name][0]:VEC_AT[name][1]]

        attn = [sb(f"attn{i}", [HEADS * SEQ]) for i in range(2)]
        ident, mean, ones = m("ident"), m("mean"), m("ones")

        b_all = psum("b_all", [2, SG, T])
        c_psum = psum("c_psum", [2, SG, T])
        bank = [psum(f"work{i}", [512]) for i in range(WORK_BANKS)]

        loaded = {n: sem(f"loaded_{n}") for n in ("vec", "x", "kv", "bv", *(a for a, _ in LOADS))}
        filled = sem("work_filled")
        used = {"act": sem("work_used_by_act"), "dve": sem("work_used_by_dve")}
        zeroed = sem("zeroed")
        small = sem("small_ready")
        a_exp = sem("a_exp_ready")
        conv_step = sem("conv_step")
        xc_ready = sem("xc_ready")
        soft_act = sem("softplus_act_step")
        soft_dve, soft_rest = sem("softplus_dve_step"), sem("softplus_rest_step")
        split = sem("split_step")
        b_ready, c_ready = sem("b_ready"), sem("c_ready")
        decay_ready = sem("decay_ready")
        c_copied = sem("c_copied")
        in_ready = sem("scan_input_ready")
        scanned = sem("scanned")
        product = {"pool": sem("output_product_pool"), "dve": sem("output_product_dve")}
        summed = sem("summed")
        rk_ready = sem("rk_ready")
        y_out = sem("mamba_y_step")
        k_ready = sem("masked_keys_ready")
        sq_ready = {k: sem(f"squares_ready_{k}") for k in ("attn", "ffn")}
        root_step = {k: sem(f"root_step_{k}") for k in ("attn", "ffn")}
        diag_ready = {k: sem(f"diag_ready_{k}") for k in ("attn", "ffn")}
        pre_ready = sem("pre_ready")
        up_ready, up_gated = sem("up_ready"), sem("up_gated")
        q_ready = sem("q_ready")
        qm_ready = sem("qmask_ready")
        rq_step = sem("rq_step")
        stored = [sem(f"stored{i}") for i in range(2)]

        block = ctx.enter_context(nc.Block())

        def tile(key):
            return bank[number[key] % WORK_BANKS]

        def wait_emptied(eng, key):
            eng.wait_ge(used[work[number[key]][1]], emptied[key])

        def wait_filled(eng, key):
            eng.wait_ge(filled, number[key] + 1)

        def wait_bank_free(eng, key):
            n = number[key]
            if n >= WORK_BANKS:
                wait_emptied(eng, work[n - WORK_BANKS][0])

        def tok(b):
            return slice(b * T, (b + 1) * T)

        def norm_kind(i):
            return "ffn" if i == 3 else "attn"

        def norm_number(b, i):
            return b + 1 if i == 3 else 2 * b + i

        def soft_rest_of(eng, engine, b):
            eng.wait_ge(soft_dve, 3 * b + 1)
            engine.tensor_tensor(trunc[:, :, :], expo[:, :, :], trunc[:, :, :], ALU.subtract).then_inc(soft_rest, 1)
            eng.wait_ge(soft_rest, 2 * b + 1)
            engine.tensor_tensor(trunc[:, :, :], pre[:, :, :], trunc[:, :, :], ALU.add).then_inc(soft_rest, 1)

        @block.sync
        def _(sp):
            def load(name, dst, src):
                sp.dma_start(dst, src).then_inc(loaded[name], 16)

            def load_mats(n):
                a, z = MAT_AT[LOADS[n][0]][0], MAT_AT[LOADS[n][1]][1]
                load(LOADS[n][0], mat[:, a:z], mats[:, a:z])

            load_mats(0)
            load("vec", vec[:, :], vecs)
            load("x", x[:, :], xT)
            for n in range(1, 3):
                load_mats(n)
            load("kv", kv[:, :], ctxT)
            load("bv", bv_row[0:1, :], bv)
            for n in range(3, len(LOADS)):
                load_mats(n)
            for b in range(BLOCKS):
                wait_emptied(sp, ("rb", b, 3))
                sp.dma_start(out[:, tok(b)], final[b % 2][:, :]).then_inc(stored[b % 2], 16)
            for i in range(2):
                sp.wait_ge(stored[i], 16 * BLOCKS // 2)

        @block.tensor
        def _(pe):
            mm = nc.tensor.matmul

            def wait_mats(*names):
                for n in names:
                    pe.wait_ge(loaded[n], 16)

            def prep():
                pe.wait_ge(zeroed, 1)
                for n in range(WARM_UP):
                    mm(c_psum[:, 0, 0, :], mid[:, 0:P], mid[:, :], start=True, stop=True)
                wait_mats("win_xT")
                out_ = tile(("wf",))
                wxT, wi = m("win_xT").rearrange("p (k n) -> p k n", k=CH), m("win_i").rearrange("p (k n) -> p k n", k=CH)
                for k in range(CH):
                    i = mm(out_[:, :], wxT[:, k, :], wi[:, k, :], start=(k == 0), stop=(k == CH - 1))
                i.then_inc(filled, 1)
                pe.wait_ge(loaded["vec"], 16)
                bias(("bf",), 0)

            def bias(key, half):
                wait_bank_free(pe, key)
                wi = m("win_i").rearrange("p (k n) -> p k n", k=CH)
                for j in range(CH):
                    for k in range(CH):
                        n = (half * CH + j) * P
                        i = mm(tile(key)[:, j:j + 1], wi[:, k, n:n + P], v("b_x")[:, k:k + 1], start=(k == 0), stop=(k == CH - 1))
                i.then_inc(filled, 1)

            def prep2():
                bias(("bfm",), 1)
                wait_mats("wxpT")
                wait_bank_free(pe, ("wxd",))
                for k in range(CH):
                    i = mm(tile(("wxd",))[:, k * INNER:(k + 1) * INNER], m("wxpT")[:, k * P:(k + 1) * P], m("wdt"), start=True, stop=True)
                i.then_inc(filled, 1)

            def xm(b):
                pe.wait_ge(loaded["x"], 16)
                wait_emptied(pe, ("wf",))
                wait_bank_free(pe, ("xm", b))
                for c in range(CH):
                    i = mm(tile(("xm", b))[:, c * T:(c + 1) * T], wf[:, c * P:(c + 1) * P], x[:, tok(b)], start=True, stop=True)
                i.then_inc(filled, 1)

            def gate(key, w):
                def part(b):
                    wait_bank_free(pe, (key, b))
                    for c in range(CH):
                        i = mm(tile((key, b))[:, c * T:(c + 1) * T], w[:, c * P:(c + 1) * P], x[:, tok(b)], start=True, stop=True)
                    i.then_inc(filled, 1)
                return part

            def delta_(b):
                pe.wait_ge(xc_ready, b + 1)
                wait_emptied(pe, ("wxd",))
                wait_bank_free(pe, ("dl", b))
                for c in range(CH):
                    for k in range(CH):
                        i = mm(tile(("dl", b))[:, c * T:(c + 1) * T], wxd[:, k, c * P:(c + 1) * P], xc[b % KEEP][:, k, :], start=(k == 0), stop=(k == CH - 1))
                i.then_inc(filled, 1)

            def bc(b):
                wbc = m("wbc").rearrange("p (k n) -> p k n", k=CH)
                wait_bank_free(pe, ("bc", b))
                for k in range(CH):
                    i = mm(tile(("bc", b))[0:PARTS * BC, 0:T], wbc[:, k, :], xc[b % KEEP][:, k, :], start=(k == 0), stop=(k == CH - 1))
                i.then_inc(filled, 1)

            def centre_w():
                wait_mats("ident", "wouto")
                wait_bank_free(pe, ("wc",))
                for k in range(CH + 1):
                    w = m("wouto")[:, k * P:(k + 1) * P] if k < CH else m("wo")
                    i = mm(tile(("wc",))[:, k * P:(k + 1) * P], w, m("centre"), start=True, stop=True)
                i.then_inc(filled, 1)
                wait_bank_free(pe, ("w3c",))
                pe.wait_ge(small, 5)
                for k in range(FT):
                    i = mm(tile(("w3c",))[:, k * P:(k + 1) * P], m("w3")[:, k * P:(k + 1) * P], s3_centre[:, :], start=True, stop=True)
                i.then_inc(filled, 1)

            def centre_x():
                wait_mats("ident")
                wait_bank_free(pe, ("bias",))
                mm(tile(("bias",))[:, 0:2], m("centre"), v("b_out_bo"), start=True, stop=True).then_inc(filled, 1)
                for n in range(TOKENS // 512):
                    wait_bank_free(pe, ("xcen", n))
                    mm(tile(("xcen", n))[:, :], m("centre"), x[:, n * 512:(n + 1) * 512], start=True, stop=True).then_inc(filled, 1)

            def scan_in(s):
                rows = PARTS * BC
                b, n = divmod(s, STEPS)
                if s == 0:
                    pe.wait_ge(small, 1)
                if n == 0:
                    pe.wait_ge(split, 5 * (b + 1))
                if s >= 2:
                    pe.wait_ge(in_ready, s - 1)
                for k in range(SG):
                    i = mm(b_all[:, s % 2, k, :], selb[0:rows, SG * n + k, None].broadcast_to([rows, P]), parts[b % KEEP][0:rows, :], start=True, stop=True)
                i.then_inc(b_ready, 1)

            def scan_c(s):
                rows = PARTS * BC
                b, n = divmod(s, STEPS)
                if s >= 2 and s % 2 == 0:
                    pe.wait_ge(c_copied, s // 2)
                elif s >= 2:
                    pe.wait_ge(product["dve"], s // 2)
                for k in range(SG):
                    i = mm(c_psum[:, s % 2, k, :], selb[0:rows, STATES + SG * n + k, None].broadcast_to([rows, P]), parts[b % KEEP][0:rows, :], start=True, stop=True)
                i.then_inc(c_ready, 1)

            def keys(b):
                pe.wait_ge(loaded["kv"], 16)
                wait_bank_free(pe, ("k", b))
                mm(tile(("k", b))[:, 0:T], m("wkT"), kv[:, tok(b)], start=True, stop=True).then_inc(filled, 1)

            def key_norm(b):
                wait_bank_free(pe, ("ssk", b))
                wait_emptied(pe, ("k", b))
                for t in range(TILES):
                    i = mm(tile(("ssk", b))[:, t * HEADS:(t + 1) * HEADS], k2[:, t * P:(t + 1) * P], m("headsel"), start=True, stop=True)
                i.then_inc(filled, 1)

            def values(b):
                pe.wait_ge(loaded["bv"], 16)
                wait_bank_free(pe, ("v", b))
                for t in range(TILES):
                    o = tile(("v", b))[:, t * P:(t + 1) * P]
                    mm(o, kv[:, b * T + t * P:b * T + (t + 1) * P], m("wvT"), start=True, stop=False)
                    i = mm(o, ones[0:1, :], bv_row[0:1, :], start=False, stop=True)
                i.then_inc(filled, 1)

            def gate_out(b):
                wait_mats("wouti")
                pe.wait_ge(y_out, Y_STEPS * (b + 1))
                w = m("wouti").rearrange("p (k n) -> p k n", k=CH)
                wait_bank_free(pe, ("oi", b))
                for c in range(CH):
                    for k in range(CH):
                        i = mm(tile(("oi", b))[:, c * T:(c + 1) * T], w[:, k, c * P:(c + 1) * P], xc[b % KEEP][:, k, :], start=(k == 0), stop=(k == CH - 1))
                i.then_inc(filled, 1)

            def proj_out(b):
                wait_bank_free(pe, ("oo", b))
                wait_emptied(pe, ("oi", b))
                wait_emptied(pe, ("wc",))
                for k in range(CH):
                    i = mm(tile(("oo", b))[:, 0:T], wouto_wo_c[:, k, :], gated[:, k, :], start=(k == 0), stop=(k == CH - 1))
                i.then_inc(filled, 1)

            def norm_var(b, i_):
                k = norm_kind(i_)
                wait_bank_free(pe, ("var", b, i_))
                pe.wait_ge(sq_ready[k], norm_number(b, i_))
                for t in range(TILES):
                    i = mm(tile(("var", b, i_))[:, t:t + 1], sq[k][:, t * P:(t + 1) * P], mean[:, 0:1], start=True, stop=True)
                i.then_inc(filled, 1)

            def norm_apply(b, i_):
                k = norm_kind(i_)
                wait_bank_free(pe, ("rb", b, i_))
                pe.wait_ge(diag_ready[k], norm_number(b, i_))
                for t in range(TILES):
                    i = mm(tile(("rb", b, i_))[:, t * P:(t + 1) * P], ones, diag[k][:, t * P:(t + 1) * P], start=True, stop=True)
                i.then_inc(filled, 1)

            def query(b):
                wait_bank_free(pe, ("q", b))
                wait_emptied(pe, ("rb", b, 1))
                mm(tile(("q", b))[:, 0:T], m("wqT"), x1[:, :], start=True, stop=True).then_inc(filled, 1)

            def query_norm(b):
                wait_bank_free(pe, ("ssq", b))
                wait_emptied(pe, ("q", b))
                for t in range(TILES):
                    i = mm(tile(("ssq", b))[:, t * HEADS:(t + 1) * HEADS], q2[:, t * P:(t + 1) * P], m("headsel"), start=True, stop=True)
                i.then_inc(filled, 1)

            def query_back(b):
                wait_bank_free(pe, ("rqb", b))
                pe.wait_ge(rq_step, 2 * (b + 1))
                for t in range(TILES):
                    i = mm(tile(("rqb", b))[:, t * P:(t + 1) * P], rq_wide[:, t * P:(t + 1) * P], ident, start=True, stop=True)
                i.then_inc(filled, 1)

            def attend(b, p):
                if p < PAIRS:
                    if p == 0:
                        pe.wait_ge(qm_ready, HI * (b + 1))
                        pe.wait_ge(k_ready, b + 1)
                    for n in range(2):
                        wait_bank_free(pe, ("s", b, p, n))
                        for g in range(2):
                            for e in range(2):
                                t = (2 * p + e) * SEQ
                                i = mm(tile(("s", b, p, n))[e * SEQ:(e + 1) * SEQ, g * HI * SEQ:(g + 1) * HI * SEQ],
                                       kmask[b % KEEP][:, 2 * n + g, t:t + SEQ], qmask[:, :, t:t + SEQ], start=True, stop=True)
                        i.then_inc(filled, 1)
                if p > 0:
                    p -= 1
                    wait_bank_free(pe, ("o", b, p))
                    if p == 0:
                        wait_emptied(pe, ("v", b))
                    for n in range(2):
                        wait_emptied(pe, ("s", b, p, n))
                    for e in range(2):
                        for i_ in range(HI):
                            for g in range(HG):
                                h = HI * g + i_
                                i = mm(tile(("o", b, p))[32 * g:32 * g + 32, e * SEQ:(e + 1) * SEQ],
                                       vmask[b % KEEP][:, p, e, g, 32 * i_:32 * i_ + 32], attn[p % 2][:, h * SEQ:(h + 1) * SEQ],
                                       start=(i_ == 0), stop=(i_ == HI - 1), skip_group_check=True)
                    i.then_inc(filled, 1)

            def attn_out(b):
                wait_bank_free(pe, ("wo", b))
                wait_emptied(pe, ("o", b, PAIRS - 1))
                wait_emptied(pe, ("wc",))
                mm(tile(("wo", b))[:, 0:T], wouto_wo_c[:, CH, :], heads_out[:, :], start=True, stop=True).then_inc(filled, 1)

            def gate_up(b, j):
                wait_mats("w1T")
                wait_emptied(pe, ("rb", b, 2))
                wait_bank_free(pe, ("gu", b, j))
                for n, w in enumerate(("w1T", "w2T")):
                    i = mm(tile(("gu", b, j))[:, n * T:(n + 1) * T], m(w)[:, j * P:(j + 1) * P], x2[b % 2][:, :], start=True, stop=True)
                i.then_inc(filled, 1)

            def hid_layer(key, w, src, before):
                w = m(w).rearrange("p (k n) -> p k n", k=FT)

                def part(b, j):
                    wait_bank_free(pe, (key, b, j))
                    for k in range(FT):
                        wait_emptied(pe, (before, b, k))
                        i = mm(tile((key, b, j))[:, 0:T], w[:, k, j * P:(j + 1) * P], src[:, k, :], start=(k == 0), stop=(k == FT - 1))
                    i.then_inc(filled, 1)
                return part

            def down(b):
                wait_bank_free(pe, ("w3", b))
                wait_emptied(pe, ("w3c",))
                for k in range(FT):
                    wait_emptied(pe, ("h2", b, k))
                    i = mm(tile(("w3", b))[:, 0:T], w3_c[:, k, :], hid_c[:, k, :], start=(k == 0), stop=(k == FT - 1))
                i.then_inc(filled, 1)

            parts_of = {"prep": prep, "prep2": prep2, "xm": xm, "gate_m": gate("zm", wf[:, INNER:2 * INNER]), "gate_z": gate("z", m("win_z")), "delta": delta_, "bc": bc, "centre_w": centre_w, "centre_x": centre_x, "scan_in": scan_in, "scan_c": scan_c, "keys": keys, "key_norm": key_norm, "values": values, "gate_out": gate_out,
                        "proj_out": proj_out, "norm_var": norm_var, "norm_apply": norm_apply, "query": query,
                        "query_norm": query_norm, "query_back": query_back, "attend": attend, "attn_out": attn_out,
                        "gate_up": gate_up, "hid1": hid_layer("h1", "h1T", hid_a, "gu"),
                        "hid2": hid_layer("h2", "h2T", hid_b, "h1"), "down": down}
            for kind, *at in steps["pe"]:
                if kind in parts_of:
                    parts_of[kind](*at)

        @block.scalar
        def _(act):
            act_ = nc.scalar.activation

            def prep():
                act.wait_ge(loaded["vec"], 16)
                act_(neg_a[:, :], v("a_log"), ACT.Exp).then_inc(a_exp, 1)
                wait_filled(act, ("wf",))
                act_(wf[:, :], tile(("wf",))[:, :], ACT.Copy).then_inc(used["act"], 1)

            def xm(b):
                if b == 0:
                    wait_emptied(act, ("bf",))
                    act.wait_ge(zeroed, 2)
                else:
                    act.wait_ge(conv_step, CH * TAPS * b)
                wait_filled(act, ("xm", b))
                for c in range(CH):
                    i = act_(xpad[:, c, :, TAPS - 1:], tile(("xm", b))[:, c * T:(c + 1) * T].rearrange("p (s t) -> p s t", t=SEQ),
                             ACT.Identity, bias=bf[:, c:c + 1])
                i.then_inc(used["act"], 1)

            def prep2():
                wait_filled(act, ("wxd",))
                act_(wxd[:, :, :].rearrange("p k n -> p (k n)"), tile(("wxd",))[:, :], ACT.Copy).then_inc(used["act"], 1)

            def centre_w():
                wait_filled(act, ("wc",))
                act_(wouto_wo_c[:, :, :].rearrange("p k n -> p (k n)"), tile(("wc",))[:, 0:(CH + 1) * P], ACT.Copy).then_inc(used["act"], 1)
                wait_filled(act, ("w3c",))
                act_(w3_c[:, :, :].rearrange("p k n -> p (k n)"), tile(("w3c",))[:, :], ACT.Copy).then_inc(used["act"], 1)

            def gate_m(b):
                if b == 0:
                    wait_emptied(act, ("bfm",))
                if b >= KEEP:
                    act.wait_ge(y_out, Y_STEPS * (b - KEEP + 1))
                wait_filled(act, ("zm", b))
                for c in range(CH):
                    i = act_(mgate[b % KEEP][:, c, :], tile(("zm", b))[:, c * T:(c + 1) * T], ACT.Silu, bias=bf[:, CH + c:CH + c + 1])
                i.then_inc(used["act"], 1)

            def gate_z(b):
                if b == 0:
                    act.wait_ge(small, 2)
                if b >= KEEP:
                    wait_emptied(act, ("oi", b - KEEP))
                wait_filled(act, ("z", b))
                for c in range(CH):
                    i = act_(zgate[b % KEEP][:, c, :], tile(("z", b))[:, c * T:(c + 1) * T], ACT.Tanh, bias=hbz[:, c:c + 1], scale=0.5)
                i.then_inc(used["act"], 1)

            def xc_(b):
                act.wait_ge(conv_step, CH * TAPS * (b + 1))
                if b >= KEEP:
                    wait_filled(act, ("oi", b - KEEP))
                act_(xc[b % KEEP][:, :, :], conv[:, :, :], ACT.Silu).then_inc(xc_ready, 1)

            def delta_(b):
                if b > 0:
                    act.wait_ge(soft_rest, 2 * b - 1)
                wait_filled(act, ("dl", b))
                for c in range(CH):
                    i = act_(expo[:, c, :], tile(("dl", b))[:, c * T:(c + 1) * T], ACT.Abs, bias=v("b_dt")[:, c:c + 1])
                i.then_inc(soft_act, 1)

            def soft(b):
                act.wait_ge(soft_act, 3 * b + 1)
                act_(expo[:, :, :], expo[:, :, :], ACT.Exp, scale=-1.0).then_inc(soft_act, 1)
                if b > 0:
                    act.wait_ge(soft_dve, 3 * b - 1)
                act.wait_ge(soft_act, 3 * b + 2)
                act_(logt[:, :, :], expo[:, :, :], ACT.Ln, bias=1.0).then_inc(soft_act, 1)
                act_(warm[:, b:b + 1], v("b_dt")[:, 0:1], ACT.Exp)

            def scan_in(s):
                b, n = divmod(s, STEPS)
                if s == 0:
                    act.wait_ge(small, 3)
                    act.wait_ge(zeroed, 3)
                if n == 0:
                    act.wait_ge(soft_dve, 3 * b + 2)
                if s >= DA_RING:
                    act.wait_ge(scanned, s - DA_RING + 1)
                for k in range(SG):
                    for c in range(CH):
                        a = c * STATES + SG * n + k
                        i = act_(decay[s % DA_RING][:, k, c, :].rearrange("p (s t) -> p s t", t=SEQ)[:, :, 1:],
                                 delta[b % KEEP][:, c, :].rearrange("p (s t) -> p s t", t=SEQ)[:, :, 1:],
                                 ACT.Exp, scale=neg_a[:, a:a + 1])
                i.then_inc(decay_ready, 1)

            def scan_c(s):
                if s % 2 == 0:
                    if s >= 4:
                        act.wait_ge(summed, s - 3)
                    act.wait_ge(c_ready, s + 1)
                    act_(c_all[s // 2 % 2][:, :, :], c_psum[:, 0, :, :], ACT.Copy).then_inc(c_copied, 1)

            def keys(b):
                if b < KEEP:
                    act.wait_ge(zeroed, 4 + 2 * b)
                else:
                    wait_filled(act, ("s", b - KEEP, PAIRS - 1, 1))
                wait_filled(act, ("k", b))
                for g in range(HG):
                    r = slice(32 * g, 32 * g + 32)
                    i = act_(kmask[b % KEEP][r, g, :], tile(("k", b))[r, 0:T], ACT.Identity, bias=v("bk")[r, :])
                i.then_inc(k_ready, 1)
                act_(k2[:, :], tile(("k", b))[:, 0:T], ACT.Square, bias=v("bk")).then_inc(used["act"], 1)

            def norm_var(b, i):
                k = norm_kind(i)
                wait_emptied(act, ({1: "oo", 2: "wo", 3: "w3"}[i], b))
                act_(sq[k][:, :], dev[k][:, :], ACT.Square).then_inc(sq_ready[k], 1)

            def query(b):
                wait_filled(act, ("q", b))
                act_(q[:, :], tile(("q", b))[:, 0:T], ACT.Identity, bias=v("bq")).then_inc(q_ready, 1)
                act_(q2[:, :], tile(("q", b))[:, 0:T], ACT.Square, bias=v("bq")).then_inc(used["act"], 1)

            def query_back(b):
                wait_filled(act, ("rqb", b))
                act_(rq_all[:, :], tile(("rqb", b))[:, 0:T], ACT.Copy).then_inc(used["act"], 1)

            def attend(b, p):
                if p == PAIRS:
                    return
                for n in range(2):
                    wait_filled(act, ("s", b, p, n))
                    if p >= 2:
                        wait_filled(act, ("o", b, p - 2))
                    act_(attn[p % 2][:, n * 512:(n + 1) * 512], tile(("s", b, p, n))[:, :], ACT.Square).then_inc(used["act"], 1)

            def gate_up(b, j):
                n = b * FT + j
                wait_filled(act, ("gu", b, j))
                if n >= 2:
                    act.wait_ge(up_gated, n - 1)
                act_(up[j % 2][:, :], tile(("gu", b, j))[:, 0:T], ACT.Tanh, scale=half_s1[:, j:j + 1]).then_inc(up_ready, 1)

            def gelu_layer(key, dst, scale):
                def part(b, j):
                    wait_filled(act, (key, b, j))
                    act_(dst[:, j, :], tile((key, b, j))[:, 0:T], ACT.Gelu, scale=v(scale)[:, j:j + 1]).then_inc(used["act"], 1)
                return part

            parts_of = {"prep": prep, "prep2": prep2, "xm": xm, "gate_m": gate_m, "gate_z": gate_z, "centre_w": centre_w, "xc": xc_, "delta": delta_, "soft": soft,
                        "scan_in": scan_in, "scan_c": scan_c, "keys": keys, "norm_var": norm_var, "query": query,
                        "query_back": query_back, "attend": attend, "gate_up": gate_up,
                        "hid1": gelu_layer("h1", hid_b, "h1s"), "hid2": gelu_layer("h2", hid_c, "h2s")}
            for kind, *at in steps["act"]:
                if kind in parts_of:
                    parts_of[kind](*at)

        @block.vector
        def _(dve):
            vec_ = nc.vector

            def prep():
                dve.wait_ge(loaded["vec"], 16)
                rows = PARTS * BC
                vec_.tensor_copy(selb[0:rows, :], v("sel")[0:rows, :]).then_inc(small, 1)
                vec_.tensor_scalar(hbz[:, :], v("b_z"), 0.5, None, ALU.mult).then_inc(small, 1)
                dve.wait_ge(a_exp, 1)
                vec_.tensor_scalar(neg_a[:, :], neg_a[:, :], -1.0, None, ALU.mult).then_inc(small, 1)
                wait_filled(dve, ("bf",))
                vec_.tensor_copy(bf[:, 0:CH], tile(("bf",))[:, 0:CH]).then_inc(used["dve"], 1)

                vec_.tensor_scalar(half_s1[:, :], v("s1"), 0.5, None, ALU.mult).then_inc(small, 1)
                dve.wait_ge(loaded["ident"], 16)
                vec_.tensor_scalar(s3_centre[:, :], m("centre"), v("s3")[:, 0:1], None, ALU.mult).then_inc(small, 1)
                dve.wait_ge(small, 4)
                vec_.tensor_tensor(half_s12[:, :], half_s1[:, :], v("s2"), ALU.mult).then_inc(small, 1)

            def prep2():
                wait_filled(dve, ("bfm",))
                vec_.tensor_copy(bf[:, CH:2 * CH], tile(("bfm",))[:, 0:CH]).then_inc(used["dve"], 1)

            def conv_(b):
                cv = conv[:, :, :].rearrange("p c (s t) -> p c s t", t=SEQ)
                w = v("conv_w").rearrange("p (c k) -> p c k", c=CH)
                wait_emptied(dve, ("xm", b))
                if b > 0:
                    dve.wait_ge(xc_ready, b)
                for c in range(CH):
                    vec_.tensor_scalar(cv[:, c], xpad[:, c, :, TAPS - 1:], w[:, c, TAPS - 1:TAPS], v("conv_b")[:, c:c + 1],
                                       ALU.mult, ALU.add).then_inc(conv_step, 1)
                for k in range(TAPS - 1):
                    for c in range(CH):
                        dve.wait_ge(conv_step, (b * TAPS + k) * CH + c + 1)
                        vec_.scalar_tensor_tensor(out=cv[:, c], in0=xpad[:, c, :, k:k + SEQ], scalar=w[:, c, k:k + 1], in1=cv[:, c],
                                                  op0=ALU.mult, op1=ALU.add).then_inc(conv_step, 1)

            def bc_(b):
                wait_filled(dve, ("bc", b))
                bc, part = tile(("bc", b)), parts[b % KEEP]
                r3, r2 = slice(0, PARTS * BC), slice(2 * BC, 3 * BC)
                if b >= KEEP:
                    dve.wait_ge(c_ready, STEPS * (b - KEEP + 1))
                vec_.tensor_copy(part[r3, :], bc[r3, 0:T]).then_inc(split, 1)
                dve.wait_ge(split, 5 * b + 1)
                vec_.tensor_tensor(bc_rest[r3, :], bc[r3, 0:T], part[r3, :], ALU.subtract).then_inc(used["dve"], 1)
                wait_emptied(dve, ("bc", b))
                vec_.tensor_copy(mid[r3, :], bc_rest[r3, :]).then_inc(split, 1)
                dve.wait_ge(split, 5 * b + 2)
                vec_.tensor_copy(part[BC:2 * BC, :], mid[BC:2 * BC, :]).then_inc(split, 1)
                vec_.tensor_tensor(bc_rest[r2, :], bc_rest[r2, :], mid[r2, :], ALU.subtract).then_inc(split, 1)
                dve.wait_ge(split, 5 * b + 4)
                vec_.tensor_copy(part[r2, :], bc_rest[r2, :]).then_inc(split, 1)

            def delta_(b):
                if b > 0:
                    dve.wait_ge(soft_rest, 2 * b)
                dve.wait_ge(soft_act, 3 * b + 1)
                for c in range(CH):
                    i = vec_.tensor_scalar(pre[:, c, :], tile(("dl", b))[:, c * T:(c + 1) * T], v("b_dt")[:, c:c + 1], 0.0,
                                           ALU.add, ALU.max)
                i.then_inc(used["dve"], 1)

            def soft(b):
                wait_emptied(dve, ("dl", b))
                dve.wait_ge(soft_act, 3 * b + 2)
                vec_.tensor_scalar(trunc[:, :, :], expo[:, :, :], 1.0, -1.0, ALU.add, ALU.add).then_inc(soft_dve, 1)
                if b == 0:
                    soft_rest_of(dve, vec_, b)

            def soft_end(b):
                d = delta[b % KEEP][:, :, :]
                dve.wait_ge(soft_rest, 2 * (b + 1))
                dve.wait_ge(soft_act, 3 * b + 3)
                vec_.tensor_tensor(d, logt[:, :, :], trunc[:, :, :], ALU.add).then_inc(soft_dve, 1)
                dve.wait_ge(soft_dve, 3 * b + 2)
                vec_.tensor_tensor(du[b % KEEP][:, :, :], d, xc[b % KEEP][:, :, :], ALU.mult).then_inc(soft_dve, 1)

            def centre_x():
                wait_filled(dve, ("bias",))
                vec_.tensor_copy(b_centred[:, :], tile(("bias",))[:, 0:2]).then_inc(used["dve"], 1)
                wait_emptied(dve, ("bias",))
                for n in range(TOKENS // 512):
                    wait_filled(dve, ("xcen", n))
                    vec_.tensor_scalar(x_centred[:, n * 512:(n + 1) * 512], tile(("xcen", n))[:, :], b_centred[:, 0:1], None, ALU.add).then_inc(used["dve"], 1)

            def scan_in(s):
                b, n = divmod(s, STEPS)
                if n == 0:
                    dve.wait_ge(soft_dve, 3 * (b + 1))
                dve.wait_ge(b_ready, s + 1)
                if s >= RING:
                    dve.wait_ge(summed, s - RING + 1)
                vec_.tensor_tensor(state[s % RING][:, :, :, :], du[b % KEEP][:, None, :, :].broadcast_to([P, SG, CH, T]),
                                   b_all[:, s % 2, :, None, :].broadcast_to([P, SG, CH, T]), ALU.mult).then_inc(in_ready, 1)

            def scan(s):
                dve.wait_ge(decay_ready, s + 1)
                dve.wait_ge(in_ready, s + 1)
                h = state[s % RING][:, :, :, :].rearrange("p k c t -> p (k c t)")
                vec_.tensor_tensor_scan(h, decay[s % DA_RING][:, :, :, :].rearrange("p k c t -> p (k c t)"), h, 0.0,
                                        ALU.mult, ALU.add).then_inc(scanned, 1)

            def scan_out(s):
                if s % 2:
                    dve.wait_ge(scanned, s + 1)
                    dve.wait_ge(c_ready, s + 1)
                    h = state[s % RING][:, :, :, :]
                    vec_.tensor_tensor(h, h, c_psum[:, 1, :, None, :].broadcast_to([P, SG, CH, T]), ALU.mult).then_inc(product["dve"], 1)

            def key_norm(b):
                wait_filled(dve, ("ssk", b))
                vec_.tensor_scalar(ssk[:, :, :].rearrange("p t h -> p (t h)"), tile(("ssk", b))[:, 0:TILES * HEADS], L2_EPS, None,
                                   ALU.add).then_inc(used["dve"], 1)
                wait_emptied(dve, ("ssk", b))
                vec_.reciprocal(rk[:, :, :], ssk[:, :, :]).then_inc(rk_ready, 1)

            def values(b):
                wait_filled(dve, ("v", b))
                dve.wait_ge(rk_ready, b + 1)
                if b < KEEP:
                    dve.wait_ge(zeroed, 5 + 2 * b)
                else:
                    wait_filled(dve, ("o", b - KEEP, PAIRS - 1))
                for p in range(PAIRS):
                    for e in range(2):
                        r = slice(e * SEQ, (e + 1) * SEQ)
                        src = tile(("v", b))[r, p * P:(p + 1) * P].rearrange("p (g i d) -> p g i d", g=HG, i=HI)
                        dst = vmask[b % KEEP][r, p, e, :, :].rearrange("p g (i w) -> p g i w", i=HI)[:, :, :, 0:DK]
                        scale = rk[r, p, :].rearrange("p (g i) -> p g i", g=HG)[:, :, :, None].broadcast_to([SEQ, HG, HI, DK])
                        i = vec_.tensor_tensor(dst, src, scale, ALU.mult)
                i.then_inc(used["dve"], 1)

            def mamba_y(b):
                dve.wait_ge(summed, STEPS * (b + 1))
                u, skip, y = xc[b % KEEP], du[b % KEEP], acc[b % 2]
                for c in range(CH):
                    vec_.scalar_tensor_tensor(out=skip[:, c, :], in0=u[:, c, :], scalar=v("d_skip")[:, c:c + 1],
                                              in1=y[:, 0, c, :], op0=ALU.mult, op1=ALU.add).then_inc(y_out, 1)
                dve.wait_ge(y_out, Y_STEPS * b + CH)
                vec_.tensor_tensor(skip[:, :, :], skip[:, :, :], y[:, 1, :, :], ALU.add).then_inc(y_out, 1)
                dve.wait_ge(y_out, Y_STEPS * b + CH + 1)
                vec_.tensor_tensor(u[:, :, :], skip[:, :, :], mgate[b % KEEP][:, :, :], ALU.mult).then_inc(y_out, 1)

            def gate_out(b):
                wait_filled(dve, ("oi", b))
                vec_.scalar_tensor_tensor(out=gated[:, :, :], in0=zgate[b % KEEP][:, :, :], scalar=1.0,
                                          in1=tile(("oi", b))[:, :].rearrange("p (c t) -> p c t", c=CH),
                                          op0=ALU.add, op1=ALU.mult).then_inc(used["dve"], 1)

            def proj_out(b):
                wait_filled(dve, ("oo", b))
                vec_.scalar_tensor_tensor(out=dev["attn"][:, :], in0=tile(("oo", b))[:, 0:T], scalar=0.5, in1=x_centred[:, tok(b)],
                                          op0=ALU.mult, op1=ALU.add).then_inc(used["dve"], 1)

            def norm_var(b, i):
                wait_filled(dve, ("var", b, i))
                k = norm_kind(i)
                vec_.tensor_scalar(var[k][:, :], tile(("var", b, i))[:, 0:TILES], LN_EPS, None, ALU.add).then_inc(used["dve"], 1)

            def norm_scale(b, i):
                k, n = norm_kind(i), (3 * ROUNDS + 1) * (norm_number(b, i) - 1)
                r, t = root[k], newton[k]
                wait_emptied(dve, ("var", b, i))
                vec_.tensor_scalar(r[:, :].bitcast(I32), var[k][:, :].bitcast(I32), -0.5, float(ROOT_GUESS), ALU.mult,
                                   ALU.add).then_inc(root_step[k], 1)
                for a in range(ROUNDS):
                    dve.wait_ge(root_step[k], n + 3 * a + 1)
                    vec_.tensor_tensor(t[:, :], r[:, :], r[:, :], ALU.mult).then_inc(root_step[k], 1)
                    dve.wait_ge(root_step[k], n + 3 * a + 2)
                    vec_.scalar_tensor_tensor(out=t[:, :], in0=t[:, :], scalar=0.25 ** a, in1=var[k][:, :], op0=ALU.mult,
                                              op1=ALU.mult).then_inc(root_step[k], 1)
                    dve.wait_ge(root_step[k], n + 3 * a + 3)
                    vec_.scalar_tensor_tensor(out=r[:, :], in0=t[:, :], scalar=-3.0, in1=r[:, :], op0=ALU.add,
                                              op1=ALU.mult).then_inc(root_step[k], 1)
                dve.wait_ge(root_step[k], n + 3 * ROUNDS + 1)
                for tt in range(TILES):
                    ins = vec_.tensor_scalar(diag[k][:, tt * P:(tt + 1) * P], ident, r[:, tt:tt + 1], (-0.5) ** ROUNDS,
                                             ALU.mult, ALU.mult)
                ins.then_inc(diag_ready[k], 1)

            def norm_apply(b, i):
                wait_filled(dve, ("rb", b, i))
                if i == 3 and b >= 2:
                    dve.wait_ge(stored[b % 2], 16 * (b // 2))
                dst = {1: x1, 2: x2[b % 2], 3: final[b % 2]}[i]
                vec_.tensor_tensor(dst[:, :], dev[norm_kind(i)][:, :], tile(("rb", b, i))[:, 0:T], ALU.mult).then_inc(used["dve"], 1)

            def query(b):
                dve.wait_ge(q_ready, b + 1)
                for i in range(HI):
                    vec_.tensor_scalar(qmask[:, i, :], q[:, :], v("hmask")[:, i:i + 1], None, ALU.mult).then_inc(qm_ready, 1)

            def query_norm(b):
                wait_filled(dve, ("ssq", b))
                vec_.tensor_scalar(ssq[:, :, :].rearrange("p t h -> p (t h)"), tile(("ssq", b))[:, 0:TILES * HEADS], L2_EPS, None,
                                   ALU.add).then_inc(used["dve"], 1)
                wait_emptied(dve, ("ssq", b))
                vec_.reciprocal(rq[:, :, :], ssq[:, :, :]).then_inc(rq_step, 1)
                dve.wait_ge(rq_step, 2 * b + 1)
                vec_.tensor_copy(rq_wide[:, :].rearrange("p (t h d) -> p t h d", h=HEADS, d=DK),
                                 rq[:, :, :, None].broadcast_to([P, TILES, HEADS, DK])).then_inc(rq_step, 1)

            def attend(b, p):
                if p == 0:
                    return
                p -= 1
                wait_filled(dve, ("o", b, p))
                wait_emptied(dve, ("rqb", b))
                vec_.tensor_tensor(heads_out[:, p * P:(p + 1) * P], tile(("o", b, p))[:, 0:P], rq_all[:, p * P:(p + 1) * P],
                                   ALU.mult).then_inc(used["dve"], 1)

            def attn_out(b):
                wait_filled(dve, ("wo", b))
                vec_.scalar_tensor_tensor(out=dev["attn"][:, :], in0=tile(("wo", b))[:, 0:T], scalar=b_centred[:, 1:2], in1=x1[:, :],
                                          op0=ALU.add, op1=ALU.add).then_inc(used["dve"], 1)

            def gate_up(b, j):
                n, ps, h = b * FT + j, tile(("gu", b, j)), hid_a[:, j, :]
                dve.wait_ge(up_ready, n + 1)
                vec_.scalar_tensor_tensor(out=h, in0=up[j % 2][:, :], scalar=1.0, in1=ps[:, 0:T], op0=ALU.add,
                                          op1=ALU.mult).then_inc(up_gated, 1)
                dve.wait_ge(up_gated, n + 1)
                vec_.scalar_tensor_tensor(out=h, in0=ps[:, T:2 * T], scalar=half_s12[:, j:j + 1], in1=h, op0=ALU.mult,
                                          op1=ALU.mult).then_inc(used["dve"], 1)

            def down(b):
                wait_filled(dve, ("w3", b))
                if b > 0:
                    wait_emptied(dve, ("rb", b - 1, 3))
                vec_.tensor_tensor(dev["ffn"][:, :], tile(("w3", b))[:, 0:T], x2[b % 2][:, :], ALU.add).then_inc(used["dve"], 1)

            parts_of = {"prep": prep, "prep2": prep2, "conv": conv_, "delta": delta_, "bc": bc_, "soft": soft, "soft_end": soft_end, "centre_x": centre_x, "scan_in": scan_in, "scan": scan, "scan_out": scan_out,
                        "key_norm": key_norm, "values": values, "mamba_y": mamba_y, "gate_out": gate_out, "proj_out": proj_out,
                        "norm_var": norm_var, "norm_scale": norm_scale, "norm_apply": norm_apply, "query": query,
                        "query_norm": query_norm, "attend": attend, "attn_out": attn_out, "gate_up": gate_up, "down": down}
            for kind, *at in steps["dve"]:
                if kind in parts_of:
                    parts_of[kind](*at)

        @block.gpsimd
        def _(pool):
            nc.gpsimd.memset(mid[:, :], 0.0).then_inc(zeroed, 1)
            nc.gpsimd.memset(xpad[:, :, :, :], 0.0).then_inc(zeroed, 1)
            for d in decay:
                i = nc.gpsimd.memset(d[:, :, :], 0.0)
            i.then_inc(zeroed, 1)
            for b in range(KEEP):
                nc.gpsimd.memset(kmask[b][:, :, :], 0.0).then_inc(zeroed, 1)
                nc.gpsimd.memset(vmask[b][:, :, :, :, :], 0.0).then_inc(zeroed, 1)

            def soft(b):
                if b > 0:
                    soft_rest_of(pool, nc.gpsimd, b)

            def scan_out(s):
                b, n = divmod(s, STEPS)
                h, y = state[s % RING][:, :, :, :], acc[b % 2][:, :, :, :]
                if s % 2 == 0:
                    pool.wait_ge(scanned, s + 1)
                    pool.wait_ge(c_copied, s // 2 + 1)
                    if n == 0 and b >= 2:
                        pool.wait_ge(y_out, Y_STEPS * (b - 1))
                    nc.gpsimd.tensor_tensor(y if n == 0 else h, h, c_all[s // 2 % 2][:, :, None, :].broadcast_to([P, SG, CH, T]),
                                            ALU.mult).then_inc(summed if n == 0 else product["pool"], 1)
                if n > 0:
                    if s % 2:
                        pool.wait_ge(product["dve"], s // 2 + 1)
                    else:
                        pool.wait_ge(product["pool"], s // 2 - b)
                    pool.wait_ge(summed, s)
                    nc.gpsimd.tensor_tensor(y, y, h, ALU.add).then_inc(summed, 1)

            parts_of = {"soft": soft, "scan_out": scan_out}
            for kind, *at in steps["pool"]:
                if kind in parts_of:
                    parts_of[kind](*at)


def kernel(**inputs):
    import concourse.bacc as bacc
    from concourse.bass_utils import run_bass_kernel_spmd

    a = {k.replace("L0_", ""): np.asarray(v) for k, v in inputs.items()}

    def rows(w):
        return np.reshape(w, (-1, P, w.shape[1])).transpose(1, 0, 2).reshape(P, -1)

    def col(w):
        return np.reshape(w, (-1, P)).T

    f = np.float32
    heads = np.arange(P) // DK
    parts = {
        "win_xT": rows(a["attn_W_in_o"][:, :INNER].T), "win_z": a["attn_W_in_o"][:, INNER:],
        "win_i": rows(a["attn_W_in_i"]), "wxpT": a["attn_W_xp"][:, :P].T, "wdt": a["attn_W_dt"],
        "wbc": rows(np.concatenate([a["attn_W_xp"][:, P:]] * PARTS, 1)),
        "ident": np.eye(P, dtype=f), "mean": np.full((P, P), 1 / P, f),
        "centre": (np.eye(P) - 1 / P).astype(f), "ones": np.ones((P, P), f),
        "headsel": (heads[:, None] == np.arange(HEADS)).astype(f),
        "wkT": a["xattn_Wk_w"].T, "wvT": a["xattn_Wv_w"].T, "wqT": a["xattn_Wq_w"].T,
        "wouti": rows(a["attn_W_out_i"]), "wouto": a["attn_W_out_o"].T, "wo": a["xattn_Wo_w"],
        "w1T": a["ffn_w1_w"].T, "w2T": a["ffn_w2_w"].T, "h1T": rows(a["ffn_h1_w"].T), "h2T": rows(a["ffn_h2_w"].T),
        "w3": a["ffn_w3_w"]}
    vectors = {
        "b_x": col(a["attn_b_in_o"][:INNER]), "b_z": col(a["attn_b_in_o"][INNER:]),
        "conv_w": rows(a["attn_conv_w"]), "conv_b": col(a["attn_conv_b"]), "b_dt": col(a["attn_b_dt"]),
        "a_log": rows(a["attn_A_log"]), "d_skip": col(a["attn_D_skip"]),
        "b_out_bo": np.stack([a["attn_b_out_o"], a["xattn_Wo_b"]], 1),
        "bq": col(a["xattn_Wq_b"]), "bk": col(a["xattn_Wk_b"]),
        "s1": col(a["ffn_w1_s"]), "s2": col(a["ffn_w2_s"]), "h1s": col(a["ffn_h1_s"]), "h2s": col(a["ffn_h2_s"]), "s3": col(a["ffn_w3_s"]),
        "hmask": (heads[:, None] % HI == np.arange(HI)).astype(f),
        "sel": (np.arange(P)[:, None] % BC == np.arange(BC)).astype(f)}
    arrays = {
        "xT": np.ascontiguousarray(a["x"].reshape(TOKENS, P).T),
        "ctxT": np.ascontiguousarray(a["ctx_1024"].reshape(TOKENS, P).T),
        "mats": np.ascontiguousarray(np.concatenate([parts[n] for n, _ in MATS], 1)),
        "vecs": np.ascontiguousarray(np.concatenate([vectors[n] for n, _ in VECS], 1)),
        "bv": np.ascontiguousarray(a["xattn_Wv_b"].reshape(1, P))}
    nc = bacc.Bacc("TRN2", target_bir_lowering=False, num_devices=1)
    args = [nc.dram_tensor(n, list(v.shape), mybir.dt.from_np(v.dtype), kind="ExternalInput").ap() for n, v in arrays.items()]
    out = nc.dram_tensor("outT", [P, TOKENS], F32, kind="ExternalOutput").ap()
    decoder_layer(nc, *args, out)
    r = run_bass_kernel_spmd(nc, [arrays], core_ids=[0])
    return r.results[0]["outT"].T.reshape(BATCH, SEQ, P)
```

```python
from contextlib import ExitStack

import concourse.bass as bass
from concourse import mybir
import numpy as np

ALU = mybir.AluOpType
AX = mybir.AxisListType
ACT = mybir.ActivationFunctionType
F32 = mybir.dt.float32
BF16 = mybir.dt.bfloat16
I32 = mybir.dt.int32

P = 128
BATCH, SEQ = 16, 64
TOKENS = BATCH * SEQ
BLOCKS = 4
T = TOKENS // BLOCKS
SEQS = T // SEQ
PAIRS = SEQS // 2
TILES = T // P
INNER = 256
CH = INNER // P
STATES = 16
SG = 2
STEPS = STATES // SG
TAPS = 4
HEADS, DK = 16, 8
HG, HI = 4, 4
HID = 512
FT = HID // P
VROW = HI * (32 + DK)
PARTS = 3
BC = 2 * STATES
WORK_BANKS = 4
RING = 4
DA_RING = 2
Y_STEPS = CH + 2
DVE_PRODUCTS = (1, 3, 5, 7)
WARM_UP = 18
KEEP = 2

MATS = [("win_xT", CH * P), ("win_i", CH * 2 * INNER), ("wxpT", INNER), ("wdt", INNER), ("win_z", INNER),
        ("wbc", CH * PARTS * BC), ("ident", P), ("mean", P), ("centre", P), ("ones", P), ("headsel", HEADS),
        ("wkT", P), ("wvT", P), ("wouto", CH * P), ("wo", P), ("w3", FT * P), ("wouti", CH * INNER), ("wqT", P),
        ("w1T", HID), ("w2T", HID), ("h1T", FT * HID), ("h2T", FT * HID)]
VECS = [("b_x", CH), ("b_z", CH), ("conv_w", CH * TAPS), ("conv_b", CH), ("b_dt", CH), ("a_log", CH * STATES),
        ("d_skip", CH), ("b_out_bo", 2), ("bq", 1), ("bk", 1), ("s1", FT), ("s2", FT), ("h1s", FT),
        ("h2s", FT), ("s3", 1), ("hmask", HI), ("sel", BC)]
LN_EPS, L2_EPS = 1e-5, 1e-8
ROUNDS = 3
ROOT_GUESS = 0x5F3759DF - (2 ** 31 + 2 ** 23) // 2


def columns(parts):
    at, n = {}, 0
    for name, w in parts:
        at[name] = (n, n + w)
        n += w
    return at, n


MAT_AT, MAT_COLS = columns(MATS)
VEC_AT, VEC_COLS = columns(VECS)
LOADS = [("win_xT", "win_i"), ("wxpT", "wbc"), ("ident", "headsel"), ("wkT", "wvT"), ("wouto", "w3"), ("wouti", "wqT"), ("w1T", "h2T")]

LANES = {
    "front": (("xm",), ("conv",), ("xc",), ("delta",), ("bc",), ("soft",), ("soft_end",)),
    "gates": (("gate_m",), ("gate_z",)),
    "kv": (("keys",), ("key_norm",), ("values",)),
    "attn": (("mamba_y",), ("gate_out",), ("proj_out",), ("norm_var", 1), ("norm_scale", 1), ("norm_apply", 1),
             ("query",), ("query_norm",), ("query_back",), ("attend", 0), ("attend", 1), ("attend", 2), ("attn_out",),
             ("norm_var", 2), ("norm_scale", 2), ("norm_apply", 2)),
    "ffn": (("gate_up", 0), ("gate_up", 1), ("gate_up", 2), ("gate_up", 3), ("hid1", 0), ("hid1", 1), ("hid1", 2),
            ("hid1", 3), ("hid2", 0), ("hid2", 1), ("hid2", 2), ("hid2", 3), ("down",), ("norm_var", 3),
            ("norm_scale", 3), ("norm_apply", 3)),
}
PLACES = {
    ("front", 0): (-14, -14, -9.5, -5.25, -4, -3.75, -3.25),
    ("front", 1): (-9.5, -7.25, -7, -4.25, -2.5, -2, -1.25),
    ("front", 2): (-5.25, -4.5, -2.25, -2, -1.5, -1.25, -0.25),
    ("front", 3): (-6.5, -4.5, -2.75, -2, -1.75, -0.5, -0.5),
    ("gates", 0): (-7.5, -6),
    ("gates", 1): (-7, -5.5),
    ("gates", 2): (-2.5, -2.5),
    ("gates", 3): (-4.75, -3.5),
    ("kv", 0): (7.25, 8.25, 8.5),
    ("kv", 1): (2.75, 7.25, 7.75),
    ("kv", 2): (11, 11.5, 12.25),
    ("kv", 3): (11, 11.25, 12),
    ("attn", 0): (11, 11.75, 12, 12.75, 13, 14, 14.25, 14.5, 15, 15, 15, 15.5, 16.5, 17, 17.25, 18),
    ("attn", 1): (10.25, 11.5, 11.75, 12.75, 13, 13.5, 13.75, 14, 14.75, 15.25, 15.25, 16, 16.75, 17, 17, 18),
    ("attn", 2): (10.25, 11.25, 11.75, 12.25, 12.75, 13.5, 14, 15, 15.25, 16, 16, 16, 16.25, 17.25, 17.25, 17.5),
    ("attn", 3): (9.75, 10.25, 11, 12.25, 12.25, 13.5, 13.5, 14.5, 15.25, 15.25, 15.25, 15.25, 15.75, 16, 16.25,
        16.75),
    ("ffn", 0): (18.5, 19.25, 19.75, 20, 21, 21.5, 21.5, 21.5, 22, 22, 23.5, 23.75, 24.75, 25, 25.75, 26.25),
    ("ffn", 1): (18.5, 19.5, 19.75, 20.25, 21.25, 21.25, 21.5, 21.5, 22, 22, 22.25, 24.25, 25.5, 26, 27, 27.75),
    ("ffn", 2): (18, 18, 20, 20, 20.75, 21, 21.75, 23.25, 24, 24.75, 24.75, 25, 26, 27.5, 28, 36),
    ("ffn", 3): (17, 17, 17.25, 17.5, 18, 19.25, 21, 21, 24.25, 26, 28.25, 28.5, 30, 30, 31.25, 32.25),
}
SCAN_PLACES = {"scan_in": 0, "scan_c": 1, "scan": 1, "scan_out": 1.75}
ONCE_PLACES = {"prep": -20, "prep2": -10, "centre_x": 1.25, "centre_w": -0.25}
LATER = {
    "act": {"xm": -0.5, "delta": 0.25, "bc": -0.75, "soft": -0.25, "gate_m": 0.25, "gate_z": 0.25, "keys": -0.5,
           "scan_c": 0.5, "norm_var": -0.5},
    "dve": {"delta": 0.25, "soft": -0.25, "soft_end": 0.5, "key_norm": -0.25, "values": 0.25, "scan_in": 0.25,
           "query": 0.75},
    "pool": {"soft": -0.25, "soft_end": -0.25, "query": -1},
}


def schedule():
    places = [(s + at, (name, s)) for name, at in SCAN_PLACES.items() for s in range(BLOCKS * STEPS)]
    places += [(at, (name,)) for name, at in ONCE_PLACES.items()]
    for b in range(BLOCKS):
        for lane, names in LANES.items():
            for (kind, *which), at in zip(names, PLACES[lane, b], strict=True):
                if kind != "attend" or which[0] <= PAIRS:
                    places.append((at + STEPS * b, (kind, b, *which)))
    return {engine: [step for _, _, step in sorted((at + LATER.get(engine, {}).get(step[0], 0), n, step)
                                                   for n, (at, step) in enumerate(places))]
            for engine in ("pe", "act", "dve", "pool")}


def work_tiles(step):
    kind, *at = step
    b = at[0] if at else 0
    if kind == "prep":
        return [(("wf",), "act"), (("bf",), "dve")]
    if kind == "prep2":
        return [(("bfm",), "dve"), (("wxd",), "act")]
    if kind == "centre_w":
        return [(("wc",), "act"), (("w3c",), "act")]
    if kind == "centre_x":
        return [(("bias",), "dve")] + [(("xcen", n), "dve") for n in range(TOKENS // 512)]
    if kind == "attend":
        p = at[1]
        return [(("s", b, p, n), "act") for n in range(2) if p < PAIRS] + [(("o", b, p - 1), "dve")] * (p > 0)
    tiles = {"xm": [("xm", "act")], "gate_m": [("zm", "act")], "gate_z": [("z", "act")],
             "delta": [("dl", "dve")], "bc": [("bc", "dve")], "keys": [("k", "act")], "key_norm": [("ssk", "dve")],
             "values": [("v", "dve")], "gate_out": [("oi", "dve")], "proj_out": [("oo", "dve")],
             "norm_var": [("var", "dve")], "norm_apply": [("rb", "dve")], "query": [("q", "act")],
             "query_norm": [("ssq", "dve")], "query_back": [("rqb", "act")], "attn_out": [("wo", "dve")],
             "gate_up": [("gu", "dve")], "hid1": [("h1", "act")], "hid2": [("h2", "act")], "down": [("w3", "dve")]}
    return [((name, *at), engine) for name, engine in tiles.get(kind, [])]


def decoder_layer(nc, xT, ctxT, mats, vecs, bv, out):
    steps = schedule()
    work = [w for step in steps["pe"] for w in work_tiles(step)]
    number = {key: n for n, (key, _) in enumerate(work)}
    emptied = {}
    for engine in ("act", "dve"):
        keys_of = [key for step in steps[engine] for key, by in work_tiles(step) if by == engine]
        emptied.update((key, n + 1) for n, key in enumerate(keys_of))

    with ExitStack() as ctx:
        def sb(name, shape, dt=F32):
            return ctx.enter_context(nc.sbuf_tensor(name, [P, *shape], dt))

        def psum(name, shape):
            return ctx.enter_context(nc.psum_tensor(name, [P, *shape], F32))

        def sem(name):
            return ctx.enter_context(nc.semaphore(name))

        mat = sb("mat", [MAT_COLS])
        vec = sb("vec", [VEC_COLS])
        bv_row = sb("bv_row", [P])
        s3_centre = sb("s3_centre", [P])
        x = sb("x", [TOKENS])
        kv = sb("kv", [TOKENS])
        wf = sb("wf", [2 * INNER])
        wxd = sb("wxd", [CH, INNER])
        bf = sb("bf", [2 * CH])
        half_bz = sb("half_bz", [CH])
        neg_a = sb("neg_a", [CH * STATES])
        selb = sb("selb", [BC], BF16)
        xpad = sb("xpad", [CH, SEQS, TAPS - 1 + SEQ])
        xc, zgate, mgate, delta, du = ([sb(f"{n}{b}", [CH, T]) for b in range(KEEP)]
                                       for n in ("xc", "zgate", "mgate", "delta", "du"))
        parts = [sb(f"parts{b}", [T], BF16) for b in range(KEEP)]
        mid = sb("mid", [T], BF16)
        decay = [sb(f"decay{i}", [SG, CH, T]) for i in range(DA_RING)]
        state = [sb(f"state{i}", [SG, CH, T]) for i in range(RING)]
        c_all = [sb(f"c_all{i}", [SG, T]) for i in range(2)]
        acc = [sb(f"acc{i}", [SG, CH, T]) for i in range(2)]
        kmask = [sb(f"kmask{b}", [HG, T]) for b in range(KEEP)]
        vmask = [sb(f"vmask{b}", [PAIRS, 2, HG, VROW]) for b in range(KEEP)]
        warm = sb("warm", [BLOCKS])
        ssk, rk, ssq, rq = (sb(n, [TILES, HEADS]) for n in ("ssk", "rk", "ssq", "rq"))
        x_centred = sb("x_centred", [TOKENS])
        b_centred = sb("b_centred", [2])
        wouto_wo_c = sb("wouto_wo_c", [CH + 1, P])
        w3_c = sb("w3_c", [FT, P])
        conv, pre, expo, logt, trunc, gated = (sb(n, [CH, T]) for n in ("conv", "pre", "expo", "logt", "trunc", "gated"))
        hid_a, hid_b, hid_c = (sb(n, [FT, T]) for n in ("hid_a", "hid_b", "hid_c"))
        qmask = sb("qmask", [HI, T])
        up = [sb(f"up{i}", [T]) for i in range(2)]
        half_s1, half_s12 = sb("half_s1", [FT]), sb("half_s12", [FT])
        dev, sq, diag = ({k: sb(f"{n}_{k}", [T]) for k in ("attn", "ffn")} for n in ("dev", "sq", "diag"))
        var, root, newton = ({k: sb(f"{n}_{k}", [TILES]) for k in ("attn", "ffn")} for n in ("var", "root", "newton"))
        k2, x1, q, q2, heads_out, rq_all, rq_wide = (sb(n, [T]) for n in ("k2", "x1", "q", "q2", "heads_out", "rq_all", "rq_wide"))
        x2 = [sb(f"x2_{i}", [T]) for i in range(2)]
        final = [sb(f"final{i}", [T]) for i in range(2)]
        bc_rest = sb("bc_rest", [T])

        def m(name):
            return mat[:, MAT_AT[name][0]:MAT_AT[name][1]]

        def v(name):
            return vec[:, VEC_AT[name][0]:VEC_AT[name][1]]

        attn = [sb(f"attn{i}", [HEADS * SEQ]) for i in range(2)]
        ident, mean, ones = m("ident"), m("mean"), m("ones")

        b_all = psum("b_all", [2, SG, T])
        c_psum = psum("c_psum", [2, SG, T])
        bank = [psum(f"work{i}", [512]) for i in range(WORK_BANKS)]

        loaded = {n: sem(f"loaded_{n}") for n in ("vec", "x", "kv", "bv", *(a for a, _ in LOADS))}
        filled = sem("work_filled")
        used = {"act": sem("work_used_by_act"), "dve": sem("work_used_by_dve")}
        zeroed = sem("zeroed")
        small = sem("small_ready")
        a_exp = sem("a_exp_ready")
        conv_step = sem("conv_step")
        xc_ready = sem("xc_ready")
        soft_act = sem("softplus_act_step")
        soft_step, soft_rest = sem("softplus_step"), sem("softplus_rest_step")
        split = sem("split_step")
        b_ready, c_ready = sem("b_ready"), sem("c_ready")
        decay_ready = sem("decay_ready")
        c_copied = sem("c_copied")
        in_ready = sem("scan_input_ready")
        scanned = sem("scanned")
        product = {"pool": sem("output_product_pool"), "dve": sem("output_product_dve")}
        summed = sem("summed")
        rk_ready = sem("rk_ready")
        y_out = sem("mamba_y_step")
        k_ready = sem("masked_keys_ready")
        sq_ready = {k: sem(f"squares_ready_{k}") for k in ("attn", "ffn")}
        root_step = {k: sem(f"root_step_{k}") for k in ("attn", "ffn")}
        diag_ready = {k: sem(f"diag_ready_{k}") for k in ("attn", "ffn")}
        pre_ready = sem("pre_ready")
        up_ready, up_gated = sem("up_ready"), sem("up_gated")
        q_ready = sem("q_ready")
        qm_ready = sem("qmask_ready")
        rq_step = sem("rq_step")
        stored = [sem(f"stored{i}") for i in range(2)]

        block = ctx.enter_context(nc.Block())

        def tile(key):
            return bank[number[key] % WORK_BANKS]

        def wait_emptied(eng, key):
            eng.wait_ge(used[work[number[key]][1]], emptied[key])

        def wait_filled(eng, key):
            eng.wait_ge(filled, number[key] + 1)

        def wait_bank_free(eng, key):
            n = number[key]
            if n >= WORK_BANKS:
                wait_emptied(eng, work[n - WORK_BANKS][0])

        def tok(b):
            return slice(b * T, (b + 1) * T)

        def norm_kind(i):
            return "ffn" if i == 3 else "attn"

        def norm_number(b, i):
            return b + 1 if i == 3 else 2 * b + i

        def by_dve(s):
            return s % STEPS in DVE_PRODUCTS

        def products(s):
            return sum(by_dve(r) == by_dve(s) for r in range(s + 1))

        def soft_end_of(eng, engine, b):
            d = delta[b % KEEP][:, :, :]
            eng.wait_ge(soft_rest, 2 * (b + 1))
            eng.wait_ge(soft_act, 3 * b + 3)
            engine.tensor_tensor(d, logt[:, :, :], trunc[:, :, :], ALU.add).then_inc(soft_step, 1)
            if b >= KEEP:
                eng.wait_ge(y_out, Y_STEPS * (b - KEEP + 1))
            eng.wait_ge(soft_step, 3 * b + 2)
            engine.tensor_tensor(du[b % KEEP][:, :, :], d, xc[b % KEEP][:, :, :], ALU.mult).then_inc(soft_step, 1)

        def mask_queries(eng, engine, b):
            eng.wait_ge(q_ready, b + 1)
            engine.tensor_tensor(qmask[:, :, :], q[:, None, :].broadcast_to([P, HI, T]), v("hmask")[:, :, None].broadcast_to([P, HI, T]),
                                 ALU.mult).then_inc(qm_ready, 1)

        def soft_rest_of(eng, engine, b):
            eng.wait_ge(soft_step, 3 * b + 1)
            engine.tensor_tensor(trunc[:, :, :], expo[:, :, :], trunc[:, :, :], ALU.subtract).then_inc(soft_rest, 1)
            eng.wait_ge(soft_rest, 2 * b + 1)
            engine.tensor_tensor(trunc[:, :, :], pre[:, :, :], trunc[:, :, :], ALU.add).then_inc(soft_rest, 1)

        @block.sync
        def _(sp):
            def load(name, dst, src):
                sp.dma_start(dst, src).then_inc(loaded[name], 16)

            def load_mats(n):
                a, z = MAT_AT[LOADS[n][0]][0], MAT_AT[LOADS[n][1]][1]
                load(LOADS[n][0], mat[:, a:z], mats[:, a:z])

            load_mats(0)
            load("vec", vec[:, :], vecs)
            load("x", x[:, :], xT)
            for n in range(1, 3):
                load_mats(n)
            load("kv", kv[:, :], ctxT)
            load("bv", bv_row[0:1, :], bv)
            for n in range(3, len(LOADS)):
                load_mats(n)
            for b in range(BLOCKS):
                wait_emptied(sp, ("rb", b, 3))
                sp.dma_start(out[:, tok(b)], final[b % 2][:, :]).then_inc(stored[b % 2], 16)
            for i in range(2):
                sp.wait_ge(stored[i], 16 * BLOCKS // 2)

        @block.tensor
        def _(pe):
            mm = nc.tensor.matmul

            def wait_mats(*names):
                for n in names:
                    pe.wait_ge(loaded[n], 16)

            def prep():
                pe.wait_ge(zeroed, 1)
                for n in range(WARM_UP):
                    mm(c_psum[:, 0, 0, :], mid[:, 0:P], mid[:, :], start=True, stop=True)
                wait_mats("win_xT")
                out_ = tile(("wf",))
                wxT, wi = m("win_xT").rearrange("p (k n) -> p k n", k=CH), m("win_i").rearrange("p (k n) -> p k n", k=CH)
                for k in range(CH):
                    i = mm(out_[:, :], wxT[:, k, :], wi[:, k, :], start=(k == 0), stop=(k == CH - 1))
                i.then_inc(filled, 1)
                pe.wait_ge(loaded["vec"], 16)
                bias(("bf",), 0)

            def bias(key, half):
                wait_bank_free(pe, key)
                wi = m("win_i").rearrange("p (k n) -> p k n", k=CH)
                for j in range(CH):
                    for k in range(CH):
                        n = (half * CH + j) * P
                        i = mm(tile(key)[:, j:j + 1], wi[:, k, n:n + P], v("b_x")[:, k:k + 1], start=(k == 0), stop=(k == CH - 1))
                i.then_inc(filled, 1)

            def prep2():
                bias(("bfm",), 1)
                wait_mats("wxpT")
                wait_bank_free(pe, ("wxd",))
                for k in range(CH):
                    i = mm(tile(("wxd",))[:, k * INNER:(k + 1) * INNER], m("wxpT")[:, k * P:(k + 1) * P], m("wdt"), start=True, stop=True)
                i.then_inc(filled, 1)

            def xm(b):
                pe.wait_ge(loaded["x"], 16)
                wait_emptied(pe, ("wf",))
                wait_bank_free(pe, ("xm", b))
                for c in range(CH):
                    i = mm(tile(("xm", b))[:, c * T:(c + 1) * T], wf[:, c * P:(c + 1) * P], x[:, tok(b)], start=True, stop=True)
                i.then_inc(filled, 1)

            def gate(key, w):
                def part(b):
                    wait_bank_free(pe, (key, b))
                    for c in range(CH):
                        i = mm(tile((key, b))[:, c * T:(c + 1) * T], w[:, c * P:(c + 1) * P], x[:, tok(b)], start=True, stop=True)
                    i.then_inc(filled, 1)
                return part

            def delta_(b):
                pe.wait_ge(xc_ready, b + 1)
                wait_emptied(pe, ("wxd",))
                wait_bank_free(pe, ("dl", b))
                for c in range(CH):
                    for k in range(CH):
                        i = mm(tile(("dl", b))[:, c * T:(c + 1) * T], wxd[:, k, c * P:(c + 1) * P], xc[b % KEEP][:, k, :], start=(k == 0), stop=(k == CH - 1))
                i.then_inc(filled, 1)

            def bc(b):
                wbc = m("wbc").rearrange("p (k n) -> p k n", k=CH)
                wait_bank_free(pe, ("bc", b))
                for k in range(CH):
                    i = mm(tile(("bc", b))[0:PARTS * BC, 0:T], wbc[:, k, :], xc[b % KEEP][:, k, :], start=(k == 0), stop=(k == CH - 1))
                i.then_inc(filled, 1)

            def centre_w():
                wait_mats("ident", "wouto")
                wait_bank_free(pe, ("wc",))
                for k in range(CH + 1):
                    w = m("wouto")[:, k * P:(k + 1) * P] if k < CH else m("wo")
                    i = mm(tile(("wc",))[:, k * P:(k + 1) * P], w, m("centre"), start=True, stop=True)
                i.then_inc(filled, 1)
                wait_bank_free(pe, ("w3c",))
                pe.wait_ge(small, 5)
                for k in range(FT):
                    i = mm(tile(("w3c",))[:, k * P:(k + 1) * P], m("w3")[:, k * P:(k + 1) * P], s3_centre[:, :], start=True, stop=True)
                i.then_inc(filled, 1)

            def centre_x():
                wait_mats("ident")
                wait_bank_free(pe, ("bias",))
                mm(tile(("bias",))[:, 0:2], m("centre"), v("b_out_bo"), start=True, stop=True).then_inc(filled, 1)
                for n in range(TOKENS // 512):
                    wait_bank_free(pe, ("xcen", n))
                    mm(tile(("xcen", n))[:, :], m("centre"), x[:, n * 512:(n + 1) * 512], start=True, stop=True).then_inc(filled, 1)

            def scan_in(s):
                rows = PARTS * BC
                b, n = divmod(s, STEPS)
                if s == 0:
                    pe.wait_ge(small, 1)
                if n == 0:
                    pe.wait_ge(split, 5 * (b + 1))
                if s >= 2:
                    pe.wait_ge(in_ready, s - 1)
                for k in range(SG):
                    i = mm(b_all[:, s % 2, k, :], selb[0:rows, SG * n + k, None].broadcast_to([rows, P]), parts[b % KEEP][0:rows, :], start=True, stop=True)
                i.then_inc(b_ready, 1)

            def scan_c(s):
                rows = PARTS * BC
                b, n = divmod(s, STEPS)
                if s >= 2 and by_dve(s - 2):
                    pe.wait_ge(product["dve"], products(s - 2))
                elif s >= 2:
                    pe.wait_ge(c_copied, products(s - 2))
                for k in range(SG):
                    i = mm(c_psum[:, s % 2, k, :], selb[0:rows, STATES + SG * n + k, None].broadcast_to([rows, P]), parts[b % KEEP][0:rows, :], start=True, stop=True)
                i.then_inc(c_ready, 1)

            def keys(b):
                pe.wait_ge(loaded["kv"], 16)
                wait_bank_free(pe, ("k", b))
                mm(tile(("k", b))[:, 0:T], m("wkT"), kv[:, tok(b)], start=True, stop=True).then_inc(filled, 1)

            def key_norm(b):
                wait_bank_free(pe, ("ssk", b))
                wait_emptied(pe, ("k", b))
                for t in range(TILES):
                    i = mm(tile(("ssk", b))[:, t * HEADS:(t + 1) * HEADS], k2[:, t * P:(t + 1) * P], m("headsel"), start=True, stop=True)
                i.then_inc(filled, 1)

            def values(b):
                pe.wait_ge(loaded["bv"], 16)
                wait_bank_free(pe, ("v", b))
                for t in range(TILES):
                    o = tile(("v", b))[:, t * P:(t + 1) * P]
                    mm(o, kv[:, b * T + t * P:b * T + (t + 1) * P], m("wvT"), start=True, stop=False)
                    i = mm(o, ones[0:1, :], bv_row[0:1, :], start=False, stop=True)
                i.then_inc(filled, 1)

            def gate_out(b):
                wait_mats("wouti")
                pe.wait_ge(y_out, Y_STEPS * (b + 1))
                w = m("wouti").rearrange("p (k n) -> p k n", k=CH)
                wait_bank_free(pe, ("oi", b))
                for c in range(CH):
                    for k in range(CH):
                        i = mm(tile(("oi", b))[:, c * T:(c + 1) * T], w[:, k, c * P:(c + 1) * P], xc[b % KEEP][:, k, :], start=(k == 0), stop=(k == CH - 1))
                i.then_inc(filled, 1)

            def proj_out(b):
                wait_bank_free(pe, ("oo", b))
                wait_emptied(pe, ("oi", b))
                wait_emptied(pe, ("wc",))
                for k in range(CH):
                    i = mm(tile(("oo", b))[:, 0:T], wouto_wo_c[:, k, :], gated[:, k, :], start=(k == 0), stop=(k == CH - 1))
                i.then_inc(filled, 1)

            def norm_var(b, i_):
                k = norm_kind(i_)
                wait_bank_free(pe, ("var", b, i_))
                pe.wait_ge(sq_ready[k], norm_number(b, i_))
                for t in range(TILES):
                    i = mm(tile(("var", b, i_))[:, t:t + 1], sq[k][:, t * P:(t + 1) * P], mean[:, 0:1], start=True, stop=True)
                i.then_inc(filled, 1)

            def norm_apply(b, i_):
                k = norm_kind(i_)
                wait_bank_free(pe, ("rb", b, i_))
                pe.wait_ge(diag_ready[k], norm_number(b, i_))
                for t in range(TILES):
                    i = mm(tile(("rb", b, i_))[:, t * P:(t + 1) * P], ones, diag[k][:, t * P:(t + 1) * P], start=True, stop=True)
                i.then_inc(filled, 1)

            def query(b):
                wait_bank_free(pe, ("q", b))
                wait_emptied(pe, ("rb", b, 1))
                mm(tile(("q", b))[:, 0:T], m("wqT"), x1[:, :], start=True, stop=True).then_inc(filled, 1)

            def query_norm(b):
                wait_bank_free(pe, ("ssq", b))
                wait_emptied(pe, ("q", b))
                for t in range(TILES):
                    i = mm(tile(("ssq", b))[:, t * HEADS:(t + 1) * HEADS], q2[:, t * P:(t + 1) * P], m("headsel"), start=True, stop=True)
                i.then_inc(filled, 1)

            def query_back(b):
                wait_bank_free(pe, ("rqb", b))
                pe.wait_ge(rq_step, 2 * (b + 1))
                for t in range(TILES):
                    i = mm(tile(("rqb", b))[:, t * P:(t + 1) * P], rq_wide[:, t * P:(t + 1) * P], ident, start=True, stop=True)
                i.then_inc(filled, 1)

            def attend(b, p):
                if p < PAIRS:
                    if p == 0:
                        pe.wait_ge(qm_ready, b + 1)
                        pe.wait_ge(k_ready, b + 1)
                    for n in range(2):
                        wait_bank_free(pe, ("s", b, p, n))
                        for g in range(2):
                            for e in range(2):
                                t = (2 * p + e) * SEQ
                                i = mm(tile(("s", b, p, n))[e * SEQ:(e + 1) * SEQ, g * HI * SEQ:(g + 1) * HI * SEQ],
                                       kmask[b % KEEP][:, 2 * n + g, t:t + SEQ], qmask[:, :, t:t + SEQ], start=True, stop=True)
                        i.then_inc(filled, 1)
                if p > 0:
                    p -= 1
                    wait_bank_free(pe, ("o", b, p))
                    if p == 0:
                        wait_emptied(pe, ("v", b))
                    for n in range(2):
                        wait_emptied(pe, ("s", b, p, n))
                    for e in range(2):
                        for i_ in range(HI):
                            for g in range(HG):
                                h = HI * g + i_
                                i = mm(tile(("o", b, p))[32 * g:32 * g + 32, e * SEQ:(e + 1) * SEQ],
                                       vmask[b % KEEP][:, p, e, g, 32 * i_:32 * i_ + 32], attn[p % 2][:, h * SEQ:(h + 1) * SEQ],
                                       start=(i_ == 0), stop=(i_ == HI - 1), skip_group_check=True)
                    i.then_inc(filled, 1)

            def attn_out(b):
                wait_bank_free(pe, ("wo", b))
                wait_emptied(pe, ("o", b, PAIRS - 1))
                wait_emptied(pe, ("wc",))
                mm(tile(("wo", b))[:, 0:T], wouto_wo_c[:, CH, :], heads_out[:, :], start=True, stop=True).then_inc(filled, 1)

            def gate_up(b, j):
                wait_mats("w1T")
                wait_emptied(pe, ("rb", b, 2))
                wait_bank_free(pe, ("gu", b, j))
                for n, w in enumerate(("w1T", "w2T")):
                    i = mm(tile(("gu", b, j))[:, n * T:(n + 1) * T], m(w)[:, j * P:(j + 1) * P], x2[b % 2][:, :], start=True, stop=True)
                i.then_inc(filled, 1)

            def hid_layer(key, w, src, before):
                w = m(w).rearrange("p (k n) -> p k n", k=FT)

                def part(b, j):
                    wait_bank_free(pe, (key, b, j))
                    for k in range(FT):
                        wait_emptied(pe, (before, b, k))
                        i = mm(tile((key, b, j))[:, 0:T], w[:, k, j * P:(j + 1) * P], src[:, k, :], start=(k == 0), stop=(k == FT - 1))
                    i.then_inc(filled, 1)
                return part

            def down(b):
                wait_bank_free(pe, ("w3", b))
                wait_emptied(pe, ("w3c",))
                for k in range(FT):
                    wait_emptied(pe, ("h2", b, k))
                    i = mm(tile(("w3", b))[:, 0:T], w3_c[:, k, :], hid_c[:, k, :], start=(k == 0), stop=(k == FT - 1))
                i.then_inc(filled, 1)

            parts_of = {"prep": prep, "prep2": prep2, "xm": xm, "gate_m": gate("zm", wf[:, INNER:2 * INNER]), "gate_z": gate("z", m("win_z")), "delta": delta_, "bc": bc, "centre_w": centre_w, "centre_x": centre_x, "scan_in": scan_in, "scan_c": scan_c, "keys": keys, "key_norm": key_norm, "values": values, "gate_out": gate_out,
                        "proj_out": proj_out, "norm_var": norm_var, "norm_apply": norm_apply, "query": query,
                        "query_norm": query_norm, "query_back": query_back, "attend": attend, "attn_out": attn_out,
                        "gate_up": gate_up, "hid1": hid_layer("h1", "h1T", hid_a, "gu"),
                        "hid2": hid_layer("h2", "h2T", hid_b, "h1"), "down": down}
            for kind, *at in steps["pe"]:
                if kind in parts_of:
                    parts_of[kind](*at)

        @block.scalar
        def _(act):
            act_ = nc.scalar.activation

            def prep():
                act.wait_ge(loaded["vec"], 16)
                act_(neg_a[:, :], v("a_log"), ACT.Exp).then_inc(a_exp, 1)
                wait_filled(act, ("wf",))
                act_(wf[:, :], tile(("wf",))[:, :], ACT.Copy).then_inc(used["act"], 1)

            def xm(b):
                if b == 0:
                    wait_emptied(act, ("bf",))
                    act.wait_ge(zeroed, 2)
                else:
                    act.wait_ge(conv_step, CH * TAPS * b)
                wait_filled(act, ("xm", b))
                for c in range(CH):
                    i = act_(xpad[:, c, :, TAPS - 1:], tile(("xm", b))[:, c * T:(c + 1) * T].rearrange("p (s t) -> p s t", t=SEQ),
                             ACT.Identity, bias=bf[:, c:c + 1])
                i.then_inc(used["act"], 1)

            def prep2():
                wait_filled(act, ("wxd",))
                act_(wxd[:, :, :].rearrange("p k n -> p (k n)"), tile(("wxd",))[:, :], ACT.Copy).then_inc(used["act"], 1)

            def centre_w():
                wait_filled(act, ("wc",))
                act_(wouto_wo_c[:, :, :].rearrange("p k n -> p (k n)"), tile(("wc",))[:, 0:(CH + 1) * P], ACT.Copy).then_inc(used["act"], 1)
                wait_filled(act, ("w3c",))
                act_(w3_c[:, :, :].rearrange("p k n -> p (k n)"), tile(("w3c",))[:, :], ACT.Copy).then_inc(used["act"], 1)

            def gate_m(b):
                if b == 0:
                    wait_emptied(act, ("bfm",))
                if b >= KEEP:
                    act.wait_ge(y_out, Y_STEPS * (b - KEEP + 1))
                wait_filled(act, ("zm", b))
                for c in range(CH):
                    i = act_(mgate[b % KEEP][:, c, :], tile(("zm", b))[:, c * T:(c + 1) * T], ACT.Silu, bias=bf[:, CH + c:CH + c + 1])
                i.then_inc(used["act"], 1)

            def gate_z(b):
                if b == 0:
                    act.wait_ge(small, 2)
                if b >= KEEP:
                    wait_emptied(act, ("oi", b - KEEP))
                wait_filled(act, ("z", b))
                for c in range(CH):
                    i = act_(zgate[b % KEEP][:, c, :], tile(("z", b))[:, c * T:(c + 1) * T], ACT.Tanh, bias=half_bz[:, c:c + 1], scale=0.5)
                i.then_inc(used["act"], 1)

            def xc_(b):
                act.wait_ge(conv_step, CH * TAPS * (b + 1))
                if b >= KEEP:
                    wait_filled(act, ("oi", b - KEEP))
                act_(xc[b % KEEP][:, :, :], conv[:, :, :], ACT.Silu).then_inc(xc_ready, 1)

            def delta_(b):
                if b > 0:
                    act.wait_ge(soft_rest, 2 * b - 1)
                wait_filled(act, ("dl", b))
                for c in range(CH):
                    i = act_(expo[:, c, :], tile(("dl", b))[:, c * T:(c + 1) * T], ACT.Abs, bias=v("b_dt")[:, c:c + 1])
                i.then_inc(soft_act, 1)

            def soft(b):
                act.wait_ge(soft_act, 3 * b + 1)
                act_(expo[:, :, :], expo[:, :, :], ACT.Exp, scale=-1.0).then_inc(soft_act, 1)
                if b > 0:
                    act.wait_ge(soft_step, 3 * b - 1)
                act.wait_ge(soft_act, 3 * b + 2)
                act_(logt[:, :, :], expo[:, :, :], ACT.Ln, bias=1.0).then_inc(soft_act, 1)
                act_(warm[:, b:b + 1], v("b_dt")[:, 0:1], ACT.Exp)

            def scan_in(s):
                b, n = divmod(s, STEPS)
                if s == 0:
                    act.wait_ge(small, 3)
                    act.wait_ge(zeroed, 3)
                if n == 0:
                    act.wait_ge(soft_step, 3 * b + 2)
                if s >= DA_RING:
                    act.wait_ge(scanned, s - DA_RING + 1)
                for k in range(SG):
                    for c in range(CH):
                        a = c * STATES + SG * n + k
                        i = act_(decay[s % DA_RING][:, k, c, :].rearrange("p (s t) -> p s t", t=SEQ)[:, :, 1:],
                                 delta[b % KEEP][:, c, :].rearrange("p (s t) -> p s t", t=SEQ)[:, :, 1:],
                                 ACT.Exp, scale=neg_a[:, a:a + 1])
                i.then_inc(decay_ready, 1)

            def scan_c(s):
                if not by_dve(s):
                    n = products(s) - 1
                    if n >= 2:
                        act.wait_ge(summed, [r for r in range(s) if not by_dve(r)][n - 2] + 1)
                    act.wait_ge(c_ready, s + 1)
                    act_(c_all[n % 2][:, :, :], c_psum[:, s % 2, :, :], ACT.Copy).then_inc(c_copied, 1)

            def keys(b):
                if b < KEEP:
                    act.wait_ge(zeroed, 4 + 2 * b)
                else:
                    wait_filled(act, ("s", b - KEEP, PAIRS - 1, 1))
                wait_filled(act, ("k", b))
                for g in range(HG):
                    r = slice(32 * g, 32 * g + 32)
                    i = act_(kmask[b % KEEP][r, g, :], tile(("k", b))[r, 0:T], ACT.Identity, bias=v("bk")[r, :])
                i.then_inc(k_ready, 1)
                act_(k2[:, :], tile(("k", b))[:, 0:T], ACT.Square, bias=v("bk")).then_inc(used["act"], 1)

            def norm_var(b, i):
                k = norm_kind(i)
                wait_emptied(act, ({1: "oo", 2: "wo", 3: "w3"}[i], b))
                act_(sq[k][:, :], dev[k][:, :], ACT.Square).then_inc(sq_ready[k], 1)

            def query(b):
                wait_filled(act, ("q", b))
                act_(q[:, :], tile(("q", b))[:, 0:T], ACT.Identity, bias=v("bq")).then_inc(q_ready, 1)
                act_(q2[:, :], tile(("q", b))[:, 0:T], ACT.Square, bias=v("bq")).then_inc(used["act"], 1)

            def query_back(b):
                wait_filled(act, ("rqb", b))
                act_(rq_all[:, :], tile(("rqb", b))[:, 0:T], ACT.Copy).then_inc(used["act"], 1)

            def attend(b, p):
                if p == PAIRS:
                    return
                for n in range(2):
                    wait_filled(act, ("s", b, p, n))
                    if p >= 2:
                        wait_filled(act, ("o", b, p - 2))
                    act_(attn[p % 2][:, n * 512:(n + 1) * 512], tile(("s", b, p, n))[:, :], ACT.Square).then_inc(used["act"], 1)

            def gate_up(b, j):
                n = b * FT + j
                wait_filled(act, ("gu", b, j))
                if n >= 2:
                    act.wait_ge(up_gated, n - 1)
                act_(up[j % 2][:, :], tile(("gu", b, j))[:, 0:T], ACT.Tanh, scale=half_s1[:, j:j + 1]).then_inc(up_ready, 1)

            def gelu_layer(key, dst, scale):
                def part(b, j):
                    wait_filled(act, (key, b, j))
                    act_(dst[:, j, :], tile((key, b, j))[:, 0:T], ACT.Gelu, scale=v(scale)[:, j:j + 1]).then_inc(used["act"], 1)
                return part

            parts_of = {"prep": prep, "prep2": prep2, "xm": xm, "gate_m": gate_m, "gate_z": gate_z, "centre_w": centre_w, "xc": xc_, "delta": delta_, "soft": soft,
                        "scan_in": scan_in, "scan_c": scan_c, "keys": keys, "norm_var": norm_var, "query": query,
                        "query_back": query_back, "attend": attend, "gate_up": gate_up,
                        "hid1": gelu_layer("h1", hid_b, "h1s"), "hid2": gelu_layer("h2", hid_c, "h2s")}
            for kind, *at in steps["act"]:
                if kind in parts_of:
                    parts_of[kind](*at)

        @block.vector
        def _(dve):
            vec_ = nc.vector

            def prep():
                dve.wait_ge(loaded["vec"], 16)
                rows = PARTS * BC
                vec_.tensor_copy(selb[0:rows, :], v("sel")[0:rows, :]).then_inc(small, 1)
                vec_.tensor_scalar(half_bz[:, :], v("b_z"), 0.5, None, ALU.mult).then_inc(small, 1)
                dve.wait_ge(a_exp, 1)
                vec_.tensor_scalar(neg_a[:, :], neg_a[:, :], -1.0, None, ALU.mult).then_inc(small, 1)
                wait_filled(dve, ("bf",))
                vec_.tensor_copy(bf[:, 0:CH], tile(("bf",))[:, 0:CH]).then_inc(used["dve"], 1)

                vec_.tensor_scalar(half_s1[:, :], v("s1"), 0.5, None, ALU.mult).then_inc(small, 1)
                dve.wait_ge(loaded["ident"], 16)
                vec_.tensor_scalar(s3_centre[:, :], m("centre"), v("s3")[:, 0:1], None, ALU.mult).then_inc(small, 1)
                dve.wait_ge(small, 4)
                vec_.tensor_tensor(half_s12[:, :], half_s1[:, :], v("s2"), ALU.mult).then_inc(small, 1)

            def prep2():
                wait_filled(dve, ("bfm",))
                vec_.tensor_copy(bf[:, CH:2 * CH], tile(("bfm",))[:, 0:CH]).then_inc(used["dve"], 1)

            def conv_(b):
                cv = conv[:, :, :].rearrange("p c (s t) -> p c s t", t=SEQ)
                w = v("conv_w").rearrange("p (c k) -> p c k", c=CH)
                wait_emptied(dve, ("xm", b))
                if b > 0:
                    dve.wait_ge(xc_ready, b)
                for c in range(CH):
                    vec_.tensor_scalar(cv[:, c], xpad[:, c, :, TAPS - 1:], w[:, c, TAPS - 1:TAPS], v("conv_b")[:, c:c + 1],
                                       ALU.mult, ALU.add).then_inc(conv_step, 1)
                for k in range(TAPS - 1):
                    for c in range(CH):
                        dve.wait_ge(conv_step, (b * TAPS + k) * CH + c + 1)
                        vec_.scalar_tensor_tensor(out=cv[:, c], in0=xpad[:, c, :, k:k + SEQ], scalar=w[:, c, k:k + 1], in1=cv[:, c],
                                                  op0=ALU.mult, op1=ALU.add).then_inc(conv_step, 1)

            def bc_(b):
                wait_filled(dve, ("bc", b))
                bc, part = tile(("bc", b)), parts[b % KEEP]
                r3, r2 = slice(0, PARTS * BC), slice(2 * BC, 3 * BC)
                if b >= KEEP:
                    dve.wait_ge(c_ready, STEPS * (b - KEEP + 1))
                vec_.tensor_copy(part[r3, :], bc[r3, 0:T]).then_inc(split, 1)
                dve.wait_ge(split, 5 * b + 1)
                vec_.tensor_tensor(bc_rest[r3, :], bc[r3, 0:T], part[r3, :], ALU.subtract).then_inc(used["dve"], 1)
                wait_emptied(dve, ("bc", b))
                vec_.tensor_copy(mid[r3, :], bc_rest[r3, :]).then_inc(split, 1)
                dve.wait_ge(split, 5 * b + 2)
                vec_.tensor_copy(part[BC:2 * BC, :], mid[BC:2 * BC, :]).then_inc(split, 1)
                vec_.tensor_tensor(bc_rest[r2, :], bc_rest[r2, :], mid[r2, :], ALU.subtract).then_inc(split, 1)
                dve.wait_ge(split, 5 * b + 4)
                vec_.tensor_copy(part[r2, :], bc_rest[r2, :]).then_inc(split, 1)

            def delta_(b):
                if b > 0:
                    dve.wait_ge(soft_rest, 2 * b)
                dve.wait_ge(soft_act, 3 * b + 1)
                for c in range(CH):
                    i = vec_.tensor_scalar(pre[:, c, :], tile(("dl", b))[:, c * T:(c + 1) * T], v("b_dt")[:, c:c + 1], 0.0,
                                           ALU.add, ALU.max)
                i.then_inc(used["dve"], 1)

            def soft(b):
                wait_emptied(dve, ("dl", b))
                dve.wait_ge(soft_act, 3 * b + 2)
                vec_.tensor_scalar(trunc[:, :, :], expo[:, :, :], 1.0, -1.0, ALU.add, ALU.add).then_inc(soft_step, 1)
                if b == 0:
                    soft_rest_of(dve, vec_, b)

            def soft_end(b):
                if b == 0:
                    soft_end_of(dve, vec_, b)

            def centre_x():
                wait_filled(dve, ("bias",))
                vec_.tensor_copy(b_centred[:, :], tile(("bias",))[:, 0:2]).then_inc(used["dve"], 1)
                wait_emptied(dve, ("bias",))
                for n in range(TOKENS // 512):
                    wait_filled(dve, ("xcen", n))
                    vec_.tensor_scalar(x_centred[:, n * 512:(n + 1) * 512], tile(("xcen", n))[:, :], b_centred[:, 0:1], None, ALU.add).then_inc(used["dve"], 1)

            def scan_in(s):
                b, n = divmod(s, STEPS)
                if n == 0:
                    dve.wait_ge(soft_step, 3 * (b + 1))
                dve.wait_ge(b_ready, s + 1)
                if s >= RING:
                    dve.wait_ge(summed, s - RING + 1)
                vec_.tensor_tensor(state[s % RING][:, :, :, :], du[b % KEEP][:, None, :, :].broadcast_to([P, SG, CH, T]),
                                   b_all[:, s % 2, :, None, :].broadcast_to([P, SG, CH, T]), ALU.mult).then_inc(in_ready, 1)

            def scan(s):
                dve.wait_ge(decay_ready, s + 1)
                dve.wait_ge(in_ready, s + 1)
                h = state[s % RING][:, :, :, :].rearrange("p k c t -> p (k c t)")
                vec_.tensor_tensor_scan(h, decay[s % DA_RING][:, :, :, :].rearrange("p k c t -> p (k c t)"), h, 0.0,
                                        ALU.mult, ALU.add).then_inc(scanned, 1)

            def scan_out(s):
                if by_dve(s):
                    dve.wait_ge(scanned, s + 1)
                    dve.wait_ge(c_ready, s + 1)
                    h = state[s % RING][:, :, :, :]
                    vec_.tensor_tensor(h, h, c_psum[:, s % 2, :, None, :].broadcast_to([P, SG, CH, T]), ALU.mult).then_inc(product["dve"], 1)

            def key_norm(b):
                wait_filled(dve, ("ssk", b))
                vec_.tensor_scalar(ssk[:, :, :].rearrange("p t h -> p (t h)"), tile(("ssk", b))[:, 0:TILES * HEADS], L2_EPS, None,
                                   ALU.add).then_inc(used["dve"], 1)
                wait_emptied(dve, ("ssk", b))
                vec_.reciprocal(rk[:, :, :], ssk[:, :, :]).then_inc(rk_ready, 1)

            def values(b):
                wait_filled(dve, ("v", b))
                dve.wait_ge(rk_ready, b + 1)
                if b < KEEP:
                    dve.wait_ge(zeroed, 5 + 2 * b)
                else:
                    wait_filled(dve, ("o", b - KEEP, PAIRS - 1))
                for p in range(PAIRS):
                    for e in range(2):
                        r = slice(e * SEQ, (e + 1) * SEQ)
                        src = tile(("v", b))[r, p * P:(p + 1) * P].rearrange("p (g i d) -> p g i d", g=HG, i=HI)
                        dst = vmask[b % KEEP][r, p, e, :, :].rearrange("p g (i w) -> p g i w", i=HI)[:, :, :, 0:DK]
                        scale = rk[r, p, :].rearrange("p (g i) -> p g i", g=HG)[:, :, :, None].broadcast_to([SEQ, HG, HI, DK])
                        i = vec_.tensor_tensor(dst, src, scale, ALU.mult)
                i.then_inc(used["dve"], 1)

            def mamba_y(b):
                dve.wait_ge(summed, STEPS * (b + 1))
                u, skip, y = xc[b % KEEP], du[b % KEEP], acc[b % 2]
                for c in range(CH):
                    vec_.scalar_tensor_tensor(out=skip[:, c, :], in0=u[:, c, :], scalar=v("d_skip")[:, c:c + 1],
                                              in1=y[:, 0, c, :], op0=ALU.mult, op1=ALU.add).then_inc(y_out, 1)
                dve.wait_ge(y_out, Y_STEPS * b + CH)
                vec_.tensor_tensor(skip[:, :, :], skip[:, :, :], y[:, 1, :, :], ALU.add).then_inc(y_out, 1)
                dve.wait_ge(y_out, Y_STEPS * b + CH + 1)
                vec_.tensor_tensor(u[:, :, :], skip[:, :, :], mgate[b % KEEP][:, :, :], ALU.mult).then_inc(y_out, 1)

            def gate_out(b):
                wait_filled(dve, ("oi", b))
                vec_.scalar_tensor_tensor(out=gated[:, :, :], in0=zgate[b % KEEP][:, :, :], scalar=1.0,
                                          in1=tile(("oi", b))[:, :].rearrange("p (c t) -> p c t", c=CH),
                                          op0=ALU.add, op1=ALU.mult).then_inc(used["dve"], 1)

            def proj_out(b):
                wait_filled(dve, ("oo", b))
                vec_.scalar_tensor_tensor(out=dev["attn"][:, :], in0=tile(("oo", b))[:, 0:T], scalar=0.5, in1=x_centred[:, tok(b)],
                                          op0=ALU.mult, op1=ALU.add).then_inc(used["dve"], 1)

            def norm_var(b, i):
                wait_filled(dve, ("var", b, i))
                k = norm_kind(i)
                vec_.tensor_scalar(var[k][:, :], tile(("var", b, i))[:, 0:TILES], LN_EPS, -0.5, ALU.add, ALU.mult).then_inc(used["dve"], 1)

            def norm_scale(b, i):
                k = norm_kind(i)
                n = ((TILES + 1) * ROUNDS + 1) * (norm_number(b, i) - 1)
                r, t, v_ = root[k], newton[k], var[k]
                wait_emptied(dve, ("var", b, i))
                vec_.tensor_scalar(r[:, :].bitcast(I32), v_[:, :].bitcast(I32), -0.5, float(ROOT_GUESS), ALU.mult,
                                   ALU.add).then_inc(root_step[k], 1)
                for a in range(ROUNDS):
                    dve.wait_ge(root_step[k], n + (TILES + 1) * a + 1)
                    for c in range(TILES):
                        c = slice(c, c + 1)
                        vec_.scalar_tensor_tensor(out=t[:, c], in0=r[:, c], scalar=v_[:, c], in1=r[:, c], op0=ALU.mult,
                                                  op1=ALU.mult).then_inc(root_step[k], 1)
                    dve.wait_ge(root_step[k], n + (TILES + 1) * (a + 1))
                    vec_.scalar_tensor_tensor(out=r[:, :], in0=t[:, :], scalar=1.5, in1=r[:, :], op0=ALU.add,
                                              op1=ALU.mult).then_inc(root_step[k], 1)
                dve.wait_ge(root_step[k], n + (TILES + 1) * ROUNDS + 1)
                for tt in range(TILES):
                    ins = vec_.tensor_scalar(diag[k][:, tt * P:(tt + 1) * P], ident, r[:, tt:tt + 1], None, ALU.mult)
                ins.then_inc(diag_ready[k], 1)

            def norm_apply(b, i):
                wait_filled(dve, ("rb", b, i))
                if i == 3 and b >= 2:
                    dve.wait_ge(stored[b % 2], 16 * (b // 2))
                dst = {1: x1, 2: x2[b % 2], 3: final[b % 2]}[i]
                vec_.tensor_tensor(dst[:, :], dev[norm_kind(i)][:, :], tile(("rb", b, i))[:, 0:T], ALU.mult).then_inc(used["dve"], 1)

            def query(b):
                if b == BLOCKS - 1:
                    mask_queries(dve, vec_, b)

            def query_norm(b):
                wait_filled(dve, ("ssq", b))
                vec_.tensor_scalar(ssq[:, :, :].rearrange("p t h -> p (t h)"), tile(("ssq", b))[:, 0:TILES * HEADS], L2_EPS, None,
                                   ALU.add).then_inc(used["dve"], 1)
                wait_emptied(dve, ("ssq", b))
                vec_.reciprocal(rq[:, :, :], ssq[:, :, :]).then_inc(rq_step, 1)
                dve.wait_ge(rq_step, 2 * b + 1)
                vec_.tensor_copy(rq_wide[:, :].rearrange("p (t h d) -> p t h d", h=HEADS, d=DK),
                                 rq[:, :, :, None].broadcast_to([P, TILES, HEADS, DK])).then_inc(rq_step, 1)

            def attend(b, p):
                if p == 0:
                    return
                p -= 1
                wait_filled(dve, ("o", b, p))
                wait_emptied(dve, ("rqb", b))
                vec_.tensor_tensor(heads_out[:, p * P:(p + 1) * P], tile(("o", b, p))[:, 0:P], rq_all[:, p * P:(p + 1) * P],
                                   ALU.mult).then_inc(used["dve"], 1)

            def attn_out(b):
                wait_filled(dve, ("wo", b))
                vec_.scalar_tensor_tensor(out=dev["attn"][:, :], in0=tile(("wo", b))[:, 0:T], scalar=b_centred[:, 1:2], in1=x1[:, :],
                                          op0=ALU.add, op1=ALU.add).then_inc(used["dve"], 1)

            def gate_up(b, j):
                n, ps, h = b * FT + j, tile(("gu", b, j)), hid_a[:, j, :]
                dve.wait_ge(up_ready, n + 1)
                vec_.scalar_tensor_tensor(out=h, in0=up[j % 2][:, :], scalar=1.0, in1=ps[:, 0:T], op0=ALU.add,
                                          op1=ALU.mult).then_inc(up_gated, 1)
                dve.wait_ge(up_gated, n + 1)
                vec_.scalar_tensor_tensor(out=h, in0=ps[:, T:2 * T], scalar=half_s12[:, j:j + 1], in1=h, op0=ALU.mult,
                                          op1=ALU.mult).then_inc(used["dve"], 1)

            def down(b):
                wait_filled(dve, ("w3", b))
                if b > 0:
                    wait_emptied(dve, ("rb", b - 1, 3))
                vec_.tensor_tensor(dev["ffn"][:, :], tile(("w3", b))[:, 0:T], x2[b % 2][:, :], ALU.add).then_inc(used["dve"], 1)

            parts_of = {"prep": prep, "prep2": prep2, "conv": conv_, "delta": delta_, "bc": bc_, "soft": soft, "soft_end": soft_end, "centre_x": centre_x, "scan_in": scan_in, "scan": scan, "scan_out": scan_out,
                        "key_norm": key_norm, "values": values, "mamba_y": mamba_y, "gate_out": gate_out, "proj_out": proj_out,
                        "norm_var": norm_var, "norm_scale": norm_scale, "norm_apply": norm_apply, "query": query,
                        "query_norm": query_norm, "attend": attend, "attn_out": attn_out, "gate_up": gate_up, "down": down}
            for kind, *at in steps["dve"]:
                if kind in parts_of:
                    parts_of[kind](*at)

        @block.gpsimd
        def _(pool):
            nc.gpsimd.memset(mid[:, :], 0.0).then_inc(zeroed, 1)
            nc.gpsimd.memset(xpad[:, :, :, :], 0.0).then_inc(zeroed, 1)
            for d in decay:
                i = nc.gpsimd.memset(d[:, :, :], 0.0)
            i.then_inc(zeroed, 1)
            for b in range(KEEP):
                nc.gpsimd.memset(kmask[b][:, :, :], 0.0).then_inc(zeroed, 1)
                nc.gpsimd.memset(vmask[b][:, :, :, :, :], 0.0).then_inc(zeroed, 1)

            def soft(b):
                if b > 0:
                    soft_rest_of(pool, nc.gpsimd, b)

            def scan_out(s):
                b, n = divmod(s, STEPS)
                h, y = state[s % RING][:, :, :, :], acc[b % 2][:, :, :, :]
                if not by_dve(s):
                    pool.wait_ge(scanned, s + 1)
                    pool.wait_ge(c_copied, products(s))
                    if n == 0 and b >= 2:
                        pool.wait_ge(y_out, Y_STEPS * (b - 1))
                    nc.gpsimd.tensor_tensor(y if n == 0 else h, h, c_all[(products(s) - 1) % 2][:, :, None, :].broadcast_to([P, SG, CH, T]),
                                            ALU.mult).then_inc(summed if n == 0 else product["pool"], 1)
                if n > 0:
                    if by_dve(s):
                        pool.wait_ge(product["dve"], products(s))
                    else:
                        pool.wait_ge(product["pool"], products(s) - b - 1)
                    pool.wait_ge(summed, s)
                    nc.gpsimd.tensor_tensor(y, y, h, ALU.add).then_inc(summed, 1)

            def soft_end(b):
                if b > 0:
                    soft_end_of(pool, nc.gpsimd, b)

            def query(b):
                if b < BLOCKS - 1:
                    mask_queries(pool, nc.gpsimd, b)

            parts_of = {"soft": soft, "soft_end": soft_end, "scan_out": scan_out, "query": query}
            for kind, *at in steps["pool"]:
                if kind in parts_of:
                    parts_of[kind](*at)


def kernel(**inputs):
    import concourse.bacc as bacc
    from concourse.bass_utils import run_bass_kernel_spmd

    a = {k.replace("L0_", ""): np.asarray(v) for k, v in inputs.items()}

    def rows(w):
        return np.reshape(w, (-1, P, w.shape[1])).transpose(1, 0, 2).reshape(P, -1)

    def col(w):
        return np.reshape(w, (-1, P)).T

    f = np.float32
    heads = np.arange(P) // DK
    parts = {
        "win_xT": rows(a["attn_W_in_o"][:, :INNER].T), "win_z": a["attn_W_in_o"][:, INNER:],
        "win_i": rows(a["attn_W_in_i"]), "wxpT": a["attn_W_xp"][:, :P].T, "wdt": a["attn_W_dt"],
        "wbc": rows(np.concatenate([a["attn_W_xp"][:, P:]] * PARTS, 1)),
        "ident": np.eye(P, dtype=f), "mean": np.full((P, P), 1 / P, f),
        "centre": (np.eye(P) - 1 / P).astype(f), "ones": np.ones((P, P), f),
        "headsel": (heads[:, None] == np.arange(HEADS)).astype(f),
        "wkT": a["xattn_Wk_w"].T, "wvT": a["xattn_Wv_w"].T, "wqT": a["xattn_Wq_w"].T,
        "wouti": rows(a["attn_W_out_i"]), "wouto": a["attn_W_out_o"].T, "wo": a["xattn_Wo_w"],
        "w1T": a["ffn_w1_w"].T, "w2T": a["ffn_w2_w"].T, "h1T": rows(a["ffn_h1_w"].T), "h2T": rows(a["ffn_h2_w"].T),
        "w3": a["ffn_w3_w"]}
    vectors = {
        "b_x": col(a["attn_b_in_o"][:INNER]), "b_z": col(a["attn_b_in_o"][INNER:]),
        "conv_w": rows(a["attn_conv_w"]), "conv_b": col(a["attn_conv_b"]), "b_dt": col(a["attn_b_dt"]),
        "a_log": rows(a["attn_A_log"]), "d_skip": col(a["attn_D_skip"]),
        "b_out_bo": np.stack([a["attn_b_out_o"], a["xattn_Wo_b"]], 1),
        "bq": col(a["xattn_Wq_b"]), "bk": col(a["xattn_Wk_b"]),
        "s1": col(a["ffn_w1_s"]), "s2": col(a["ffn_w2_s"]), "h1s": col(a["ffn_h1_s"]), "h2s": col(a["ffn_h2_s"]), "s3": col(a["ffn_w3_s"]),
        "hmask": (heads[:, None] % HI == np.arange(HI)).astype(f),
        "sel": (np.arange(P)[:, None] % BC == np.arange(BC)).astype(f)}
    arrays = {
        "xT": np.ascontiguousarray(a["x"].reshape(TOKENS, P).T),
        "ctxT": np.ascontiguousarray(a["ctx_1024"].reshape(TOKENS, P).T),
        "mats": np.ascontiguousarray(np.concatenate([parts[n] for n, _ in MATS], 1)),
        "vecs": np.ascontiguousarray(np.concatenate([vectors[n] for n, _ in VECS], 1)),
        "bv": np.ascontiguousarray(a["xattn_Wv_b"].reshape(1, P))}
    nc = bacc.Bacc("TRN2", target_bir_lowering=False, num_devices=1)
    args = [nc.dram_tensor(n, list(v.shape), mybir.dt.from_np(v.dtype), kind="ExternalInput").ap() for n, v in arrays.items()]
    out = nc.dram_tensor("outT", [P, TOKENS], F32, kind="ExternalOutput").ap()
    decoder_layer(nc, *args, out)
    r = run_bass_kernel_spmd(nc, [arrays], core_ids=[0])
    return r.results[0]["outT"].T.reshape(BATCH, SEQ, P)
```
